# Optimizing a Trainium2 kernel written in Bass

```python
import numpy as np
import jax
import jax.numpy as jnp

def _softmax(x, axis=-1):
    return jax.nn.softmax(x, axis=axis)

def _gelu(x):
    return jax.nn.gelu(x, approximate=True)

def _silu(x):
    return jax.nn.silu(x)

def _sigmoid(x):
    return jax.nn.sigmoid(x)

def _layernorm(x, axis=-1, eps=1e-05):
    m = jnp.mean(x, axis=axis, keepdims=True)
    v = jnp.var(x, axis=axis, keepdims=True)
    return (x - m) / jnp.sqrt(v + eps)

def _scatter_add(tgt, idx, src, axis=0):
    return tgt.at[idx].add(src)

def _segment_sum(src, seg, n):
    return jax.ops.segment_sum(src, seg, n)
kernel_name = 'mk_gnn_resnorm_d1_gnn_r8_dc64ba'

def setup_inputs(seed: int=0):
    np.random.seed(seed)
    _w = jnp.asarray

    def _rec_inputs():
        import jax
        import jax.numpy as jnp
        _gk = jax.random.key(seed)
        x = -0.001812 + 1 * jax.random.normal(jax.random.fold_in(_gk, 1), (12500, 32), jnp.float32)
        _s = jax.random.randint(jax.random.fold_in(_gk, 2), (200000,), 0, 12500, jnp.int32)
        _d = jax.random.randint(jax.random.fold_in(_gk, 3), (200000,), 0, 12500, jnp.int32)
        _loop = jnp.arange(12500, dtype=jnp.int32)
        src = jnp.concatenate([_s, _d, _loop])
        dst = jnp.concatenate([_d, _s, _loop])
        _o = jnp.argsort(dst, stable=True)
        src = src[_o]
        dst = dst[_o]
        edge_attr_10 = jax.random.uniform(jax.random.fold_in(_gk, 12), (412500, 10), jnp.float32, 0.0, 0.999998)
        edge_attr_3 = 0.00158508 + 0.999651 * jax.random.normal(jax.random.fold_in(_gk, 13), (412500, 3), jnp.float32)
        edge_weight = jax.random.uniform(jax.random.fold_in(_gk, 14), (412500,), jnp.float32, 0.0, 0.999997)
        return (x, src, dst, edge_attr_10, edge_attr_3, edge_weight)
    x, src, dst, edge_attr_10, edge_attr_3, edge_weight = _rec_inputs()

    def _L0_gnn_setup():
        import jax, jax.numpy as jnp
        import numpy as np
        SQRT3 = 3.0 ** 0.5

        def _mlp(emb, w1, w2):
            h = jax.nn.relu(emb @ w1 / jnp.sqrt(jnp.float32(w1.shape[0])))
            return h @ w2 / jnp.sqrt(jnp.float32(w2.shape[0]))
        key = jax.random.key(seed)
        ks = jax.random.split(key, 10)
        N, E = (1250, 20000)
        x = jax.random.normal(ks[0], (N, 32), jnp.float32)
        edge_src = jax.random.randint(ks[1], (E,), 0, N)
        edge_dst = jax.random.randint(ks[2], (E,), 0, N)
        edge_vec = jax.random.normal(ks[3], (E, 3), jnp.float32)
        emb = jax.random.uniform(ks[4], (E, 10), jnp.float32)
        norm = jax.random.uniform(ks[5], (E,), jnp.float32)
        fc1_w1 = jax.random.normal(ks[6], (10, 16), jnp.float32)
        fc1_w2 = jax.random.normal(ks[7], (16, 512), jnp.float32)
        fc2_w1 = jax.random.normal(ks[8], (10, 16), jnp.float32)
        fc2_w2 = jax.random.normal(ks[9], (16, 384), jnp.float32)
        return dict(x=x, edge_src=edge_src, edge_dst=edge_dst, edge_vec=edge_vec, emb=emb, norm=norm, num_nodes=N, fc1_w1=fc1_w1, fc1_w2=fc1_w2, fc2_w1=fc2_w1, fc2_w2=fc2_w2)
    _L0_gnn_all = _L0_gnn_setup()
    _L0_gnn_in = {k: v for k, v in _L0_gnn_all.items() if k in ('fc1_w1', 'fc1_w2', 'fc2_w1', 'fc2_w2')}
    del _L0_gnn_all
    return {'x': x, 'src': src, 'dst': dst, 'edge_attr_10': edge_attr_10, 'edge_attr_3': edge_attr_3, 'edge_weight': edge_weight, 'L0_gnn_fc1_w1': _L0_gnn_in['fc1_w1'], 'L0_gnn_fc1_w2': _L0_gnn_in['fc1_w2'], 'L0_gnn_fc2_w1': _L0_gnn_in['fc2_w1'], 'L0_gnn_fc2_w2': _L0_gnn_in['fc2_w2']}

def reference(x, src, dst, edge_attr_10, edge_attr_3, edge_weight, L0_gnn_fc1_w1, L0_gnn_fc1_w2, L0_gnn_fc2_w1, L0_gnn_fc2_w2):
    import jax
    import jax.numpy as jnp

    def _L0_gnn_ref(x, edge_src, edge_dst, edge_vec, emb, norm, num_nodes, fc1_w1, fc1_w2, fc2_w1, fc2_w2):
        import jax, jax.numpy as jnp
        import numpy as np
        SQRT3 = 3.0 ** 0.5

        def _mlp(emb, w1, w2):
            h = jax.nn.relu(emb @ w1 / jnp.sqrt(jnp.float32(w1.shape[0])))
            return h @ w2 / jnp.sqrt(jnp.float32(w2.shape[0]))
        E = edge_vec.shape[0]
        r = edge_vec / jnp.linalg.norm(edge_vec, axis=1, keepdims=True)
        sh1 = SQRT3 * r
        xs, xd = (x[edge_src], x[edge_dst])
        s1 = jnp.concatenate([xs[:, :8], xd[:, :8]], axis=1)
        v1 = jnp.concatenate([xs[:, 8:].reshape(E, 8, 3), xd[:, 8:].reshape(E, 8, 3)], axis=1)
        w = _mlp(emb, fc1_w1, fc1_w2)
        Wss = w[:, 0:128].reshape(E, 16, 8)
        Wvv = w[:, 128:256].reshape(E, 16, 8)
        Wsv = w[:, 256:384].reshape(E, 16, 8)
        Wvs = w[:, 384:512].reshape(E, 16, 8)
        a1 = 1.0 / jnp.sqrt(32.0)
        vdot1 = jnp.einsum('euk,ek->eu', v1, sh1) / SQRT3
        s_t = a1 * (jnp.einsum('eu,euw->ew', s1, Wss) + jnp.einsum('eu,euw->ew', vdot1, Wvv))
        v_t = a1 * (jnp.einsum('eu,euw->ew', s1, Wsv)[:, :, None] * sh1[:, None, :] + jnp.einsum('euk,euw->ewk', v1, Wvs))
        w2 = _mlp(emb, fc2_w1, fc2_w2)
        Ass = w2[:, 0:64].reshape(E, 8, 8)
        Avv = w2[:, 64:128].reshape(E, 8, 8)
        Bss = w2[:, 128:192].reshape(E, 8, 8)
        Bvv = w2[:, 192:256].reshape(E, 8, 8)
        Csv = w2[:, 256:320].reshape(E, 8, 8)
        Cvs = w2[:, 320:384].reshape(E, 8, 8)
        a2 = 1.0 / jnp.sqrt(16.0)
        vdot2 = jnp.einsum('euk,ek->eu', v_t, sh1) / SQRT3
        scal = a2 * (jnp.einsum('eu,euw->ew', s_t, Ass) + jnp.einsum('eu,euw->ew', vdot2, Avv))
        gates = a2 * (jnp.einsum('eu,euw->ew', s_t, Bss) + jnp.einsum('eu,euw->ew', vdot2, Bvv))
        vecs = a2 * (jnp.einsum('eu,euw->ew', s_t, Csv)[:, :, None] * sh1[:, None, :] + jnp.einsum('euk,euw->ewk', v_t, Cvs))
        edge_out = jnp.concatenate([jnp.tanh(scal), (vecs * jnp.tanh(gates)[:, :, None]).reshape(E, 24)], axis=1)
        edge_out = edge_out * norm[:, None]
        return jax.ops.segment_sum(edge_out, edge_dst, num_segments=num_nodes)
    x = _layernorm(x + _L0_gnn_ref(x, src, dst, edge_attr_3, edge_attr_10, edge_weight, 12500, L0_gnn_fc1_w1, L0_gnn_fc1_w2, L0_gnn_fc2_w1, L0_gnn_fc2_w2), axis=-1)
    return x

_drawn_inputs = setup_inputs


def setup_inputs(seed=0):
    import zlib

    import numpy as np

    out = dict(_drawn_inputs(seed))
    spreads = {}
    factors = {}
    for name, (base, spread) in spreads.items():
        noise = np.random.default_rng([zlib.crc32(name.encode()), seed]).standard_normal(out[name].shape)
        drawn = base * np.exp(spread * noise) if base else spread * noise
        out[name] = jnp.asarray(drawn.astype(out[name].dtype))
    for name, factor in factors.items():
        out[name] = (out[name] * factor).astype(out[name].dtype)
    return out
```

```python
from contextlib import ExitStack

import concourse.bass as bass
from concourse import mybir

P = 128
G = 8
SUPER = P * G
WINDOW = 64
C = 8
F = 32
H = 16
L1, L2 = 512, 384
PIECES = 6
KH = PIECES * H
EPS = 1e-5

ALU = mybir.AluOpType
ACT = mybir.ActivationFunctionType
AX = mybir.AxisListType
F32 = mybir.dt.float32
BF16 = mybir.dt.bfloat16
I32 = mybir.dt.int32
RMAX = bass.bass_isa.ReduceOp.max


def build_gnn_layer(nc, x, src, dst, emb_t, vec, weight, fc1_w1, fc1_w2, fc2_w1, fc2_w2, out):
    N = x.shape[0]
    E = src.shape[0]
    K1 = emb_t.shape[0]
    FULL = E // SUPER
    NS = FULL + (1 if E % SUPER else 0)
    REPEATED = NS * SUPER - E
    NB = -(-N // P)
    NW = -(-N // WINDOW)
    ACC = max(NB * P, NW * WINDOW) + WINDOW
    SCAN = -(-FULL // P)
    assert NS >= 6 and NS <= 512 and SCAN * SUPER + SUPER <= ACC

    c1 = 1.0 / (4.0 * 32.0 ** 0.5)
    c2 = 1.0 / (4.0 * 4.0)
    r3 = 3.0 ** 0.5

    def rows(ap, width):
        flat = ap[0:FULL * SUPER] if width == 1 else ap[0:FULL * SUPER, :]
        pat = "(s p t) -> s p t" if width == 1 else "(s p t) k -> s p (t k)"
        return flat.rearrange(pat, p=P, t=G)

    def last_rows(ap, width):
        flat = ap[E - SUPER:E] if width == 1 else ap[E - SUPER:E, :]
        pat = "(p t) -> p t" if width == 1 else "(p t) k -> p (t k)"
        return flat.rearrange(pat, t=G)

    src_rows, dst_rows, wgt_rows, vec_rows = rows(src, 1), rows(dst, 1), rows(weight, 1), rows(vec, 3)
    emb_cols = emb_t[:, 0:FULL * SUPER].rearrange("k (s e) -> s k e", e=SUPER)

    with ExitStack() as ctx:
        def sb(name, shape, dt=F32):
            return ctx.enter_context(nc.sbuf_tensor(name, shape, dt))

        def sem(name):
            return ctx.enter_context(nc.semaphore(name))

        identity = sb("identity", [P, P])
        identity_bf = sb("identity_bf", [P, P], BF16)
        node_iota_i = sb("node_iota_i", [P, WINDOW], I32)
        node_iota = sb("node_iota", [P, WINDOW])
        edge_iota_i = sb("edge_iota_i", [P, G], I32)
        fresh = sb("fresh", [P, G])
        minus_half = sb("minus_half", [P, G])
        ones_row = sb("ones_row", [1, P])
        w1 = sb("w1", [K1, 2 * H])
        w2 = sb("w2", [H, L1 + L2])
        w2_rest = sb("w2_rest", [H, L1 + L2])
        w2_parts = sb("w2_parts", [H, 3, L1 + L2], BF16)
        w2_stack = sb("w2_stack", [KH, L1 + L2], BF16)
        base_i = sb("base_i", [1, NS], I32)
        base_row = sb("base_row", [1, NS])
        base = sb("base", [P, NS])
        span = sb("span", [P, 3, SCAN + 1])
        excess = sb("excess", [P, SCAN + 1])
        excess_low = sb("excess_low", [P, SCAN + 1])
        excess_one = sb("excess_one", [P, 1])
        excess_all = sb("excess_all", [P, 1])
        general = sb("general", [P, 1], I32)

        idx = sb("idx", [P, 2, 2, G], I32)
        emb = sb("emb", [K1, 2, SUPER])
        vecs = sb("vecs", [P, 2, G, 3])
        late = sb("late", [P, 2, G])
        late_dst = sb("late_dst", [P, 2, G], I32)
        nodes = sb("nodes", [P, 2, G, 2, F])
        norm2 = sb("norm2", [P, G])
        vsq = sb("vsq", [P, G, 3])
        inv = sb("inv", [P, G])
        r = sb("r", [P, 2, G, 3])
        S = sb("S", [P, 2, G, 4 * C])
        V = sb("V", [P, 2, G, 3, 2 * C])
        vr = sb("vr", [P, G, 3, 2 * C])
        hid = sb("hid", [P, 2 * G, H])
        hid_rest = sb("hid_rest", [P, 2 * G, H])
        hid_parts = sb("hid_parts", [P, 2 * G, KH], BF16)
        hid_t = sb("hid_t", [KH, 3, G, P], BF16)
        wa = sb("wa", [P, G, L1])
        wb = sb("wb", [P, G, L2])
        prod_s = sb("prod_s", [P, G, 4 * C, C])
        prod_v = sb("prod_v", [P, G, 3, 2 * C, C])
        sv = sb("sv", [P, G, C])
        M = sb("M", [P, G, 2 * C])
        VT = sb("VT", [P, G, 3, C])
        vtr = sb("vtr", [P, G, 3, C])
        prod_g = sb("prod_g", [P, G, 2, 2 * C, C])
        prod_o = sb("prod_o", [P, G, 4, C, C])
        osum = sb("osum", [P, G, 4, C])
        th = sb("th", [P, G, 2, C])
        gate = sb("gate", [P, G, C])
        q = sb("q", [P, G, 3, C])
        msg = sb("msg", [P, G, F])
        rel = sb("rel", [P, 2, G])
        rel_raw = sb("rel_raw", [P, G])
        hot = sb("hot", [P, 2, G, WINDOW])
        acc = sb("acc", [P, ACC])

        xn = sb("xn", [P, NB, F])
        mean = sb("mean", [P, NB])
        var = sb("var", [P, NB])

        pw = ctx.enter_context(nc.psum_tensor("pw", [P, 2, 2, 512], F32))
        pt = ctx.enter_context(nc.psum_tensor("pt", [KH, G, P], BF16))
        ph = ctx.enter_context(nc.psum_tensor("ph", [P, 512], F32))
        p1 = ctx.enter_context(nc.psum_tensor("p1", [P, 512], F32))
        p2 = ctx.enter_context(nc.psum_tensor("p2", [P, 512], F32))
        hid_ps = ph[:, 0:G * 2 * H].rearrange("p (t h) -> p t h", h=2 * H)
        vs_ps = p1[:, 0:G * 3 * C].rearrange("p (t k w) -> p t k w", k=3, w=C)
        st_ps = p1[:, G * 3 * C:G * 4 * C].rearrange("p (t w) -> p t w", w=C)
        gates_ps = p2[:, 0:G * 2 * C].rearrange("p (t a w) -> p t a w", a=2, w=C)
        scat_ps = p2[0:F, G * 2 * C:G * 2 * C + WINDOW]

        s_const = sem("s_const")
        s_w_in = sem("s_w_in")
        s_base_in = sem("s_base_in")
        s_scan_in = sem("s_scan_in")
        s_pre = sem("s_pre")
        s_parts = sem("s_parts")
        s_stack = sem("s_stack")
        s_base_row = sem("s_base_row")
        s_base_ps = sem("s_base_ps")
        s_excess = sem("s_excess")
        s_excess_all = sem("s_excess_all")
        s_general = sem("s_general")
        idx_in = [sem(f"idx_in{i}") for i in range(2)]
        emb_in = [sem(f"emb_in{i}") for i in range(2)]
        vec_in = [sem(f"vec_in{i}") for i in range(2)]
        late_in = [sem(f"late_in{i}") for i in range(2)]
        nodes_in = [[sem(f"nodes_in{i}{k}") for k in range(2)] for i in range(2)]
        vsq_done = sem("vsq_done")
        norm2_done = sem("norm2_done")
        inv_done = sem("inv_done")
        r_done = sem("r_done")
        sv_copied = sem("sv_copied")
        vr_done = sem("vr_done")
        vdot_done = sem("vdot_done")
        hid_mm = sem("hid_mm")
        hid_done = sem("hid_done")
        hid_a = sem("hid_a")
        hid_b = sem("hid_b")
        hid_rest_done = sem("hid_rest_done")
        hid_c = sem("hid_c")
        turned = sem("turned")
        turned_out = sem("turned_out")
        wa_mm = sem("wa_mm")
        wa_out = sem("wa_out")
        wb_mm = sem("wb_mm")
        wb_out = sem("wb_out")
        pv_done = sem("pv_done")
        ps_done = sem("ps_done")
        p2_done = sem("p2_done")
        sv_done = sem("sv_done")
        vs_sum = sem("vs_sum")
        st_sum = sem("st_sum")
        m_st = sem("m_st")
        vt_part = sem("vt_part")
        vt_done = sem("vt_done")
        vtr_done = sem("vtr_done")
        m_vd = sem("m_vd")
        pg_done = sem("pg_done")
        po_done = sem("po_done")
        osum_done = sem("osum_done")
        gates_sum = sem("gates_sum")
        tanh_done = sem("tanh_done")
        gate_done = sem("gate_done")
        q_done = sem("q_done")
        msg_done = sem("msg_done")
        rel_raw_done = sem("rel_raw_done")
        rel_done = sem("rel_done")
        hot_done = sem("hot_done")
        scat_mm = sem("scat_mm")
        acc_done = sem("acc_done")
        rel_kept = sem("rel_kept")
        rel_moved = sem("rel_moved")
        gathers_begun = sem("gathers_begun")
        windows_begun_pe = sem("windows_begun_pe")
        windows_begun_dve = sem("windows_begun_dve")
        xn_in = sem("xn_in")
        turn_acc = sem("turn_acc")
        post = sem("post")
        root_done = sem("root_done")
        out_done = sem("out_done")

        class At:

            def __init__(self, b, d):
                self.b, self.par, self.half = b, d % 2, b + d // 2
                self.static = isinstance(b, int)
                self.d = d

            def n(self, per=1, more=0):
                return self.b * (2 * per) + (self.d * per + more)

            def k(self, per, more=0):
                return self.b * per + (per * (self.d // 2 + 1) + more)

            def before(self, by):
                return At(self.b, self.d - by)

            def index(self):
                return self.b * 2 + self.d

            def is_last(self):
                return self.static and 2 * self.b + self.d == NS - 1 and NS != FULL

        def wait(eng, semaphore, value):
            if isinstance(value, int) and value <= 0:
                return
            eng.wait_ge(semaphore, value)

        def periods(eng, body):
            pairs = (NS - 4) // 2
            for i in range(-1, 2):
                body(At(0, i) if i >= 0 else At(0, -1), i)
            first = 2
            with eng.Fori(0, pairs) as b:
                body(At(b + 1, 0), None)
                body(At(b + 1, 1), None)
            for i in range(first + 2 * pairs, NS + 2):
                body(At(i // 2, i % 2), i)

        def stage(at, by, i):
            if i is not None and not 0 <= i + by < NS:
                return None
            return At(at.b, at.d + by)

        block = ctx.enter_context(nc.Block())

        @block.sync
        def _(sp):
            sp.dma_start(base_i[0:1, 0:FULL], dst[0:FULL * SUPER].rearrange("(a s e) -> a s e", a=1, e=SUPER)[:, :, 0],
                         allow_slow_non_contiguous=True).then_inc(s_base_in, 16)
            if NS != FULL:
                sp.dma_start(base_i[0:1, FULL:NS], dst[E - SUPER:E - SUPER + 1].rearrange("(a s) -> a s", a=1)
                             ).then_inc(s_base_in, 16)
            scan = acc[:, :].bitcast(I32)
            for c in range(SCAN):
                n = min(P, FULL - c * P)
                sp.dma_start(scan[0:n, c * SUPER:(c + 1) * SUPER],
                             dst[c * P * SUPER:(c * P + n) * SUPER].rearrange("(s e) -> s e", e=SUPER)
                             ).then_inc(s_scan_in, 16)
            sp.dma_start(scan[0:1, SCAN * SUPER:(SCAN + 1) * SUPER],
                         dst[E - SUPER:E].rearrange("(a e) -> a e", a=1)).then_inc(s_scan_in, 16)
            sp.dma_start(w1[:, 0:H], fc1_w1).then_inc(s_w_in, 16)
            sp.dma_start(w1[:, H:2 * H], fc2_w1).then_inc(s_w_in, 16)
            sp.dma_start(w2[:, 0:L1], fc1_w2).then_inc(s_w_in, 16)
            sp.dma_start(w2[:, L1:L1 + L2], fc2_w2).then_inc(s_w_in, 16)

            def load(a):
                p, s = a.par, a.index()
                two = a.before(2)
                last = a.is_last()
                for k in range(2):
                    wait(sp, nodes_in[p][k], two.k(16 * G))
                sp.dma_start(idx[:, p, 0, :], last_rows(src, 1) if last else src_rows[s]).then_inc(idx_in[p], 16)
                sp.dma_start(idx[:, p, 1, :], last_rows(dst, 1) if last else dst_rows[s]).then_inc(idx_in[p], 16)
                wait(sp, hid_mm, two.n(1, 1))
                sp.dma_start(emb[:, p, :], emb_t[:, E - SUPER:E] if last else emb_cols[s]).then_inc(emb_in[p], 16)
                wait(sp, r_done, two.n(1, 1))
                sp.dma_start(vecs[:, p, :, :].rearrange("p t k -> p (t k)"),
                             last_rows(vec, 3) if last else vec_rows[s]).then_inc(vec_in[p], 16)

            def load_late(a):
                p, s = a.par, a.index()
                two = a.before(2)
                last = a.is_last()
                wait(sp, msg_done, two.n(2, 2))
                wait(sp, rel_raw_done, two.n(1, 1))
                sp.dma_start(late[:, p, :], last_rows(weight, 1) if last else wgt_rows[s]).then_inc(late_in[p], 16)
                sp.dma_start(late_dst[:, p, :], last_rows(dst, 1) if last else dst_rows[s]).then_inc(late_in[p], 16)

            load(At(0, 0))
            sp.wait_ge(s_parts, 1)
            for g, part in enumerate((0, 1, 2, 0, 1, 0)):
                sp.dma_start(w2_stack[H * g:H * g + H, :], w2_parts[:, part, :]).then_inc(s_stack, 16)

            def body(at, i):
                a = stage(at, 2, i)
                if a is not None:
                    load(a)
                a = stage(at, 1, i)
                if a is not None:
                    load_late(a)

            periods(sp, body)
            whole = N // NB
            sp.dma_start(xn[0:whole, :, :].rearrange("p b f -> p (b f)"),
                         x[0:whole * NB, :].rearrange("(p b) f -> p (b f)", b=NB)).then_inc(xn_in, 16)
            if N > whole * NB:
                sp.dma_start(xn[whole:whole + 1, 0:N - whole * NB, :].rearrange("p b f -> p (b f)"),
                             x[whole * NB:N, :].rearrange("(p b) f -> p (b f)", p=1)).then_inc(xn_in, 16)
            sp.wait_ge(post, 9)
            sp.dma_start(out[0:whole * NB, :].rearrange("(p b) f -> p (b f)", b=NB),
                         xn[0:whole, :, :].rearrange("p b f -> p (b f)")).then_inc(out_done, 16)
            if N > whole * NB:
                sp.dma_start(out[whole * NB:N, :].rearrange("(p b) f -> p (b f)", p=1),
                             xn[whole:whole + 1, 0:N - whole * NB, :].rearrange("p b f -> p (b f)")
                             ).then_inc(out_done, 16)
            sp.wait_ge(out_done, 32 if N > whole * NB else 16)

        @block.gpsimd
        def _(pool):
            nc.gpsimd.memset(identity[:, :], 0.0).then_inc(s_const, 1)
            nc.gpsimd.memset(identity_bf[:, :], 0.0).then_inc(s_const, 1)
            nc.gpsimd.memset(minus_half[:, :], -0.5).then_inc(s_const, 1)
            nc.gpsimd.memset(ones_row[:, :], 1.0).then_inc(s_const, 1)
            nc.gpsimd.iota(node_iota_i[:, :], pattern=[[1, WINDOW]], base=0, channel_multiplier=0).then_inc(s_const, 1)
            nc.gpsimd.iota(edge_iota_i[:, :], pattern=[[1, G]], base=0, channel_multiplier=G).then_inc(s_const, 1)
            nc.gpsimd.memset(xn[:, :, :], 0.0).then_inc(s_const, 1)
            pool.wait_ge(s_const, 7)
            for m in (identity, identity_bf):
                nc.gpsimd.affine_select(out=m[:, :], in_=m[:, :], compare_op=ALU.not_equal, fill=1.0, base=0,
                                        pattern=[[-1, P]], channel_multiplier=1).then_inc(s_const, 1)

            def gathers(a):
                p = a.par
                pool.wait_ge(idx_in[p], a.k(32))
                wait(pool, sv_copied, a.before(2).n(4, 4))
                pool.sem_inc(gathers_begun, 1)
                for side in range(2):
                    for t in range(G):
                        nc.gpsimd.indirect_dma_start(
                            nodes[:, p, t, side, :], None, x,
                            bass.IndirectOffsetOnAxis(ap=idx[:, p, side, t:t + 1], axis=0)
                        ).then_inc(nodes_in[p][side], 16)

            def inverse(a):
                pool.wait_ge(norm2_done, a.n(1, 1))
                wait(pool, r_done, a.n())
                nc.gpsimd.tensor_tensor(inv[:, :], norm2[:, :], minus_half[:, :], ALU.pow).then_inc(inv_done, 1)

            gathers(At(0, 0))
            pool.wait_ge(s_excess, 1)
            nc.gpsimd.partition_all_reduce(excess_all[:, :], excess_one[:, :], P, RMAX).then_inc(s_excess_all, 1)

            def body(at, i):
                a = stage(at, 1, i)
                if a is not None:
                    inverse(a)
                a = stage(at, 2, i)
                if a is not None:
                    gathers(a)

            periods(pool, body)

        @block.scalar
        def _(act):
            def rows_laid_out(a):
                p = a.par
                wait(act, p2_done, a.before(2).n(1, 1))
                for side in range(2):
                    act.wait_ge(nodes_in[p][side], a.k(16 * G))
                    c = slice(C * side, C * side + C)
                    nc.scalar.activation(S[:, p, :, c], nodes[:, p, :, side, 0:C], ACT.Copy).then_inc(sv_copied, 1)
                    nc.scalar.activation(V[:, p, :, :, c],
                                         nodes[:, p, :, side, C:F].rearrange("p t (u k) -> p t k u", k=3),
                                         ACT.Copy).then_inc(sv_copied, 1)

            def hidden(a):
                act.wait_ge(hid_mm, a.n(1, 1))
                wait(act, hid_rest_done, a.n())
                nc.scalar.activation(hid[:, :, :].rearrange("p (t l) h -> p t (l h)", l=2), hid_ps, ACT.Relu,
                                     scale=float(K1) ** -0.5).then_inc(hid_done, 1)
                act.wait_ge(hid_done, a.n(1, 1))
                wait(act, turned, a.n(2))
                parts = hid_parts[:, :, :].rearrange("p a (g h) -> p a g h", h=H)
                nc.scalar.activation(parts[:, :, 0:3, :], hid[:, :, :].unsqueeze(2).broadcast_to([P, 2 * G, 3, H]),
                                     ACT.Copy).then_inc(hid_a, 1)
                act.wait_ge(hid_rest_done, a.n(1, 1))
                nc.scalar.activation(parts[:, :, 3:5, :], hid_rest[:, :, :].unsqueeze(2).broadcast_to([P, 2 * G, 2, H]),
                                     ACT.Copy).then_inc(hid_b, 1)

            def turned_copies(a):
                for layer in range(2):
                    act.wait_ge(turned, a.n(2, layer + 1))
                    wait(act, (wa_mm, wb_mm)[layer], a.n(4, -4 * layer))
                    nc.scalar.activation(hid_t[:, layer and 1 + a.par, :, :], pt[:, :, :], ACT.Copy).then_inc(turned_out, 1)

            def weights_out(a, buf, width, made, taken, used):
                wait(act, used, a.n())
                for pair in range(G // 2):
                    act.wait_ge(made, a.n(4, pair + 1))
                    nc.scalar.activation(buf[:, 2 * pair:2 * pair + 2, :], pw[:, pair % 2, :, 0:width],
                                         ACT.Copy).then_inc(taken, 1)

            def tanhs(a):
                act.wait_ge(gates_sum, a.n(1, 1))
                wait(act, msg_done, a.n(2))
                nc.scalar.activation(th[:, :, :, :], gates_ps, ACT.Tanh).then_inc(tanh_done, 1)

            def body(at, i):
                one, two, three = stage(at, 1, i), stage(at, 0, i), stage(at, -1, i)
                if three is not None:
                    weights_out(three, wb, L2, wb_mm, wb_out, osum_done)
                if one is not None:
                    hidden(one)
                    turned_copies(one)
                    rows_laid_out(one)
                if three is not None:
                    tanhs(three)
                if one is not None:
                    weights_out(one, wa, L1, wa_mm, wa_out, sv_done)

            periods(act, body)
            act.wait_ge(post, 6)
            nc.scalar.activation(var[:, :], var[:, :], ACT.Sqrt).then_inc(root_done, 1)

        @block.tensor
        def _(pe):
            pe.wait_ge(s_const, 9)
            pe.wait_ge(s_base_row, 1)
            nc.tensor.matmul(ph[:, 0:NS], ones_row[:, :], base_row[:, :], start=True, stop=True).then_inc(s_base_ps, 1)
            pe.wait_ge(s_general, 1)
            pe.wait_ge(s_w_in, 64)
            pe.wait_ge(s_stack, 16 * PIECES)
            flag = nc.tensor.value_load(general[0:1, 0:1], min_val=0, max_val=1)

            def hidden(a):
                p = a.par
                pe.wait_ge(emb_in[p], a.k(16))
                wait(pe, hid_done, a.n())
                for t in range(G):
                    mm = nc.tensor.matmul(hid_ps[:, t, :], emb[:, p, t:SUPER:G], w1[:, :], start=True, stop=True)
                mm.then_inc(hid_mm, 1)

            def turn(a):
                pe.wait_ge(hid_a, a.n(1, 1))
                pe.wait_ge(hid_b, a.n(1, 1))
                pe.wait_ge(hid_c, a.n(1, 1))
                for layer in range(2):
                    wait(pe, turned_out, a.n(2, layer))
                    for t in range(G):
                        mm = nc.tensor.transpose(pt[:, t, :], hid_parts[:, 2 * t + layer, :], identity_bf[:, :])
                    mm.then_inc(turned, 1)

            def edge_weights(a, layer, other_taken):
                made, taken = ((wa_mm, wa_out), (wb_mm, wb_out))[layer]
                lo, width = ((0, L1), (L1, L2))[layer]
                pe.wait_ge(turned_out, a.n(2, layer + 1))
                wait(pe, *other_taken)
                for pair in range(G // 2):
                    if pair >= 2:
                        pe.wait_ge(taken, a.n(4, pair - 1))
                    for t in range(2):
                        mm = nc.tensor.matmul(pw[:, pair % 2, t, 0:width], hid_t[:, layer and 1 + a.par, 2 * pair + t, :],
                                              w2_stack[:, lo:lo + width], start=True, stop=True)
                    mm.then_inc(made, 1)

            def sums1(a):
                pe.wait_ge(pv_done, a.n(1, 1))
                wait(pe, vt_done, a.n())
                wait(pe, m_st, a.n())
                for u in range(2 * C):
                    mm = nc.tensor.matmul(vs_ps, identity[:, :], prod_v[:, :, :, u, :],
                                          start=(u == 0), stop=(u == 2 * C - 1))
                mm.then_inc(vs_sum, 1)
                pe.wait_ge(ps_done, a.n(1, 1))
                for u in range(4 * C):
                    mm = nc.tensor.matmul(st_ps, identity[:, :], prod_s[:, :, u, :],
                                          start=(u == 0), stop=(u == 4 * C - 1))
                mm.then_inc(st_sum, 1)

            def sums2(a, windows):
                pe.wait_ge(pg_done, a.n(1, 1))
                wait(pe, acc_done, a.n(windows))
                wait(pe, tanh_done, a.n())
                for u in range(2 * C):
                    mm = nc.tensor.matmul(gates_ps, identity[:, :], prod_g[:, :, :, u, :],
                                          start=(u == 0), stop=(u == 2 * C - 1))
                mm.then_inc(gates_sum, 1)

            def window(par):
                for t in range(G):
                    mm = nc.tensor.matmul(scat_ps, msg[:, t, :], hot[:, par, t, :], start=(t == 0), stop=(t == G - 1))
                mm.then_inc(scat_mm, 1)

            def scatter(a, is_general):
                pe.wait_ge(msg_done, a.n(2, 2))
                if not is_general:
                    pe.wait_ge(hot_done, a.n(1, 1))
                    wait(pe, acc_done, a.n())
                    window(a.par)
                    return
                pe.sem_inc(windows_begun_pe, 1)
                with pe.Fori(0, NW) as w:
                    pe.wait_ge(hot_done, a.n(NW, 1) + w)
                    pe.wait_ge(acc_done, a.n(NW) + w)
                    window(a.par)

            def program(is_general):
                def body(at, i):
                    one, two, three, four = (stage(at, by, i) for by in (1, 0, -1, -2))
                    if four is not None:
                        scatter(four, is_general)
                    if three is not None:
                        edge_weights(three, 1, (wa_out, three.n(4, 8) if two is not None else three.n(4, 4)))
                    if one is not None:
                        hidden(one)
                    if two is not None:
                        sums1(two)
                    if one is not None:
                        turn(one)
                    if three is not None:
                        sums2(three, NW if is_general else 1)
                    if one is not None:
                        edge_weights(one, 0, (wb_out, one.n(4, -4)))
                periods(pe, body)

            with pe.If(flag == 0):
                program(False)
            with pe.If(flag != 0):
                program(True)
            pe.wait_ge(acc_done, 0)
            pe.wait_ge(post, 1)
            banks = (pw[:, 0, 0, :], pw[:, 0, 1, :], pw[:, 1, 0, :], pw[:, 1, 1, :], ph[:, :], p1[:, :], p2[:, :])
            per = 512 // F
            for b in range(NB):
                mm = nc.tensor.matmul(banks[b // per][:, F * (b % per):F * (b % per) + F],
                                      acc[0:F, b:b + NB * (P - 1) + 1:NB], identity[0:F, 0:F], start=True, stop=True)
            mm.then_inc(turn_acc, 1)

        @block.vector
        def _(dve):
            steps = [0]

            def done(ins):
                steps[0] += 1
                ins.then_inc(s_pre, 1)
                dve.wait_ge(s_pre, steps[0])

            dve.wait_ge(s_w_in, 64)
            done(nc.vector.tensor_scalar(w2[:, 0:256], w2[:, 0:256], c1, None, ALU.mult))
            done(nc.vector.tensor_scalar(w2[:, 256:384], w2[:, 256:384], c1 * r3, None, ALU.mult))
            done(nc.vector.tensor_scalar(w2[:, 384:L1], w2[:, 384:L1], c1, None, ALU.mult))
            done(nc.vector.tensor_scalar(w2[:, L1:L1 + 256], w2[:, L1:L1 + 256], c2, None, ALU.mult))
            done(nc.vector.tensor_scalar(w2[:, L1 + 256:L1 + 320], w2[:, L1 + 256:L1 + 320], c2 * r3, None, ALU.mult))
            done(nc.vector.tensor_scalar(w2[:, L1 + 320:L1 + L2], w2[:, L1 + 320:L1 + L2], c2, None, ALU.mult))
            done(nc.vector.tensor_copy(w2_parts[:, 0, :], w2[:, :]))
            done(nc.vector.tensor_tensor(w2_rest[:, :], w2[:, :], w2_parts[:, 0, :], ALU.subtract))
            done(nc.vector.tensor_copy(w2_parts[:, 1, :], w2_rest[:, :]))
            nc.vector.tensor_tensor(w2_parts[:, 2, :], w2_rest[:, :], w2_parts[:, 1, :],
                                    ALU.subtract).then_inc(s_parts, 1)
            dve.wait_ge(s_base_in, 32 if NS != FULL else 16)
            nc.vector.tensor_copy(base_row[:, :], base_i[:, :]).then_inc(s_base_row, 1)
            done(nc.vector.memset(span[:, :, :], 0.0))
            dve.wait_ge(s_scan_in, 16 * (SCAN + 1))
            scan = acc[:, :].bitcast(I32)
            for c in range(SCAN + 1):
                n = min(P, FULL - c * P) if c < SCAN else 1
                part = scan[0:n, c * SUPER:(c + 1) * SUPER]
                done(nc.vector.tensor_reduce(span[0:n, 0, c:c + 1], part, AX.X, ALU.max))
                done(nc.vector.tensor_reduce(span[0:n, 1, c:c + 1], part, AX.X, ALU.min))
                done(nc.vector.tensor_copy(span[0:n, 2, c:c + 1], part[:, 0:1]))
            done(nc.vector.tensor_tensor(excess[:, :], span[:, 0, :], span[:, 2, :], ALU.subtract))
            done(nc.vector.tensor_scalar(excess[:, :], excess[:, :], -(WINDOW - 1.0), None, ALU.add))
            done(nc.vector.tensor_tensor(excess_low[:, :], span[:, 2, :], span[:, 1, :], ALU.subtract))
            done(nc.vector.tensor_tensor(excess[:, :], excess[:, :], excess_low[:, :], ALU.max))
            nc.vector.tensor_reduce(excess_one[:, :], excess[:, :], AX.X, ALU.max).then_inc(s_excess, 1)
            done(nc.vector.memset(acc[:, :], 0.0))
            dve.wait_ge(s_const, 9)
            done(nc.vector.tensor_copy(node_iota[:, :], node_iota_i[:, :]))
            done(nc.vector.tensor_scalar(fresh[:, :], edge_iota_i[:, :], float(REPEATED), None, ALU.is_ge))
            dve.wait_ge(s_base_ps, 1)
            done(nc.vector.tensor_copy(base[:, :], ph[:, 0:NS]))
            dve.wait_ge(s_excess_all, 1)
            nc.vector.tensor_scalar(general[:, :], excess_all[:, :], 0.0, None, ALU.is_gt).then_inc(s_general, 1)
            dve.wait_ge(s_general, 1)
            flag = nc.vector.value_load(general[0:1, 0:1], min_val=0, max_val=1)

            def lengths(a):
                p = a.par
                dve.wait_ge(vec_in[p], a.k(16))
                nc.vector.tensor_tensor(vsq[:, :, :], vecs[:, p, :, :], vecs[:, p, :, :], ALU.mult).then_inc(vsq_done, 1)
                dve.wait_ge(vsq_done, a.n(1, 1))
                wait(dve, inv_done, a.n())
                nc.vector.tensor_reduce(norm2[:, :], vsq[:, :, :], AX.X, ALU.add).then_inc(norm2_done, 1)

            def split(a):
                dve.wait_ge(hid_a, a.n(1, 1))
                wait(dve, hid_b, a.n())
                nc.vector.tensor_tensor(hid_rest[:, :, :], hid[:, :, :], hid_parts[:, :, 0:H],
                                        ALU.subtract).then_inc(hid_rest_done, 1)

            def split_again(a):
                dve.wait_ge(hid_b, a.n(1, 1))
                nc.vector.tensor_tensor(hid_parts[:, :, KH - H:KH], hid_rest[:, :, :], hid_parts[:, :, 3 * H:4 * H],
                                        ALU.subtract).then_inc(hid_c, 1)

            def directions(a):
                p = a.par
                dve.wait_ge(inv_done, a.n(1, 1))
                dve.wait_ge(vec_in[p], a.k(16))
                nc.vector.tensor_tensor(r[:, p, :, :], vecs[:, p, :, :],
                                        inv[:, :].unsqueeze(2).broadcast_to([P, G, 3]), ALU.mult).then_inc(r_done, 1)
                dve.wait_ge(r_done, a.n(1, 1))
                dve.wait_ge(sv_copied, a.n(4, 4))
                nc.vector.tensor_tensor(vr[:, :, :, :], V[:, p, :, :, :],
                                        r[:, p, :, :].unsqueeze(3).broadcast_to([P, G, 3, 2 * C]),
                                        ALU.mult).then_inc(vr_done, 1)

            def vdots(a):
                dve.wait_ge(vr_done, a.n(1, 1))
                nc.vector.tensor_reduce(S[:, a.par, :, 2 * C:4 * C], vr[:, :, :, :].rearrange("p t k u -> p t u k"),
                                        AX.X, ALU.add).then_inc(vdot_done, 1)

            def products1(a):
                p = a.par
                dve.wait_ge(wa_out, a.n(4, 4))
                wait(dve, vs_sum, a.n())
                nc.vector.tensor_tensor(
                    prod_v[:, :, :, :, :],
                    wa[:, :, 384:L1].rearrange("p t (u w) -> p t u w", w=C).unsqueeze(2).broadcast_to([P, G, 3, 2 * C, C]),
                    V[:, p, :, :, :].unsqueeze(4).broadcast_to([P, G, 3, 2 * C, C]), ALU.mult).then_inc(pv_done, 1)
                vdots(a)
                dve.wait_ge(vdot_done, a.n(1, 1))
                wait(dve, st_sum, a.n())
                nc.vector.tensor_tensor(
                    prod_s[:, :, :, :], wa[:, :, 0:256].rearrange("p t (u w) -> p t u w", w=C),
                    S[:, p, :, :].unsqueeze(3).broadcast_to([P, G, 4 * C, C]), ALU.mult).then_inc(ps_done, 1)
                third = wa[:, :, 256:384].rearrange("p t (u w) -> p t u w", w=C)
                nc.vector.tensor_tensor(
                    third, third, S[:, p, :, 0:2 * C].unsqueeze(3).broadcast_to([P, G, 2 * C, C]),
                    ALU.mult).then_inc(p2_done, 1)

            def sv_sum(a):
                dve.wait_ge(p2_done, a.n(1, 1))
                nc.vector.tensor_reduce(sv[:, :, :], wa[:, :, 256:384].rearrange("p t (u w) -> p t w u", w=C),
                                        AX.X, ALU.add).then_inc(sv_done, 1)

            def destinations(a, is_general):
                p = a.par
                dve.wait_ge(late_in[p], a.k(32))
                first = 0.0 if is_general else base[:, bass.ds(a.index(), 1)] if not a.static else base[:, a.index():a.index() + 1]
                nc.vector.tensor_scalar(rel_raw[:, :], late_dst[:, p, :], first, None, ALU.subtract).then_inc(rel_raw_done, 1)
                dve.wait_ge(rel_raw_done, a.n(1, 1))

            def destinations_kept(a):
                p = a.par
                if a.is_last():
                    nc.vector.scalar_tensor_tensor(rel[:, p, :], rel_raw[:, :], 1.0, fresh[:, :], ALU.add,
                                                   ALU.mult).then_inc(rel_kept, 1)
                    dve.wait_ge(rel_kept, 1)
                    nc.vector.tensor_scalar(rel[:, p, :], rel[:, p, :], -1.0, None, ALU.add).then_inc(rel_done, 1)
                else:
                    nc.vector.tensor_copy(rel[:, p, :], rel_raw[:, :]).then_inc(rel_done, 1)

            def one_hot(par):
                return nc.vector.tensor_tensor(
                    hot[:, par, :, :], node_iota[:, :].unsqueeze(1).broadcast_to([P, G, WINDOW]),
                    rel[:, par, :].unsqueeze(2).broadcast_to([P, G, WINDOW]), ALU.is_equal)

            def products2(a):
                dve.wait_ge(wb_out, a.n(4, 4))
                dve.wait_ge(m_st, a.n(1, 1))
                dve.wait_ge(m_vd, a.n(1, 1))
                wait(dve, gates_sum, a.n())
                for half in range(2):
                    ins = nc.vector.tensor_tensor(
                        prod_g[:, :, half, :, :],
                        wb[:, :, 128 * half:128 * half + 128].rearrange("p t (u w) -> p t u w", w=C),
                        M[:, :, :].unsqueeze(3).broadcast_to([P, G, 2 * C, C]), ALU.mult)
                ins.then_inc(pg_done, 1)
                nc.vector.tensor_tensor(
                    prod_o[:, :, 0:3, :, :],
                    wb[:, :, 320:L2].rearrange("p t (u w) -> p t u w", w=C).unsqueeze(2).broadcast_to([P, G, 3, C, C]),
                    VT[:, :, :, :].unsqueeze(4).broadcast_to([P, G, 3, C, C]), ALU.mult).then_inc(po_done, 1)
                nc.vector.tensor_tensor(
                    prod_o[:, :, 3, :, :], wb[:, :, 256:320].rearrange("p t (u w) -> p t u w", w=C),
                    M[:, :, 0:C].unsqueeze(3).broadcast_to([P, G, C, C]), ALU.mult).then_inc(po_done, 1)

            def sums2(a):
                dve.wait_ge(po_done, a.n(2, 2))
                nc.vector.tensor_reduce(
                    osum[:, :, :, :].rearrange("p t k w -> p (t k) w"),
                    prod_o[:, :, :, :, :].rearrange("p t k u w -> p (t k) w u"), AX.X, ALU.add).then_inc(osum_done, 1)

            def between(a):
                p = a.par
                rb = r[:, p, :, :].unsqueeze(3).broadcast_to([P, G, 3, C])
                dve.wait_ge(sv_done, a.n(1, 1))
                wait(dve, po_done, a.n(2))
                nc.vector.tensor_tensor(VT[:, :, :, :], sv[:, :, :].unsqueeze(2).broadcast_to([P, G, 3, C]), rb,
                                        ALU.mult).then_inc(vt_part, 1)
                dve.wait_ge(vs_sum, a.n(1, 1))
                dve.wait_ge(st_sum, a.n(1, 1))
                dve.wait_ge(vt_part, a.n(1, 1))
                nc.vector.tensor_tensor(VT[:, :, :, :], VT[:, :, :, :], vs_ps, ALU.add).then_inc(vt_done, 1)
                dve.wait_ge(vt_done, a.n(1, 1))
                nc.vector.tensor_tensor(vtr[:, :, :, :], VT[:, :, :, :], rb, ALU.mult).then_inc(vtr_done, 1)
                nc.vector.tensor_copy(M[:, :, 0:C], st_ps).then_inc(m_st, 1)
                dve.wait_ge(vtr_done, a.n(1, 1))
                nc.vector.tensor_reduce(M[:, :, C:2 * C], vtr[:, :, :, :].rearrange("p t k w -> p t w k"), AX.X,
                                        ALU.add).then_inc(m_vd, 1)

            def messages(a, windows):
                p = a.par
                rb = r[:, p, :, :].unsqueeze(3).broadcast_to([P, G, 3, C])
                wb_ = late[:, p, :].unsqueeze(2).broadcast_to([P, G, C])
                dve.wait_ge(osum_done, a.n(1, 1))
                nc.vector.tensor_tensor(q[:, :, :, :], osum[:, :, 3, :].unsqueeze(2).broadcast_to([P, G, 3, C]), rb,
                                        ALU.mult).then_inc(q_done, 1)
                dve.wait_ge(late_in[p], a.k(32))
                dve.wait_ge(tanh_done, a.n(1, 1))
                nc.vector.tensor_tensor(gate[:, :, :], th[:, :, 1, :], wb_, ALU.mult).then_inc(gate_done, 1)
                dve.wait_ge(q_done, a.n(2, 1))
                nc.vector.tensor_tensor(q[:, :, :, :], q[:, :, :, :], osum[:, :, 0:3, :], ALU.add).then_inc(q_done, 1)
                wait(dve, scat_mm, a.n(windows))
                nc.vector.tensor_tensor(msg[:, :, 0:C], th[:, :, 0, :], wb_, ALU.mult).then_inc(msg_done, 1)
                dve.wait_ge(q_done, a.n(2, 2))
                dve.wait_ge(gate_done, a.n(1, 1))
                nc.vector.tensor_tensor(
                    msg[:, :, C:F].rearrange("p t (w k) -> p t k w", k=3), q[:, :, :, :],
                    gate[:, :, :].unsqueeze(2).broadcast_to([P, G, 3, C]), ALU.mult).then_inc(msg_done, 1)

            def add_window(first):
                cols = acc[0:F, bass.ds(first, WINDOW)]
                return nc.vector.tensor_tensor(cols, cols, scat_ps, ALU.add)

            def scatter(a, is_general):
                if not is_general:
                    dve.wait_ge(scat_mm, a.n(1, 1))
                    wait(dve, acc_done, a.n())
                    first = nc.vector.value_load(base_i[0:1, bass.ds(a.index(), 1)], min_val=0, max_val=N - 1)
                    add_window(first).then_inc(acc_done, 1)
                    return
                dve.wait_ge(rel_done, a.n(1, 1))
                dve.sem_inc(windows_begun_dve, 1)
                with dve.Fori(0, NW) as w:
                    dve.wait_ge(scat_mm, a.n(NW) + w)
                    dve.wait_ge(rel_moved, a.n(NW) + w)
                    one_hot(a.par).then_inc(hot_done, 1)
                    dve.wait_ge(hot_done, a.n(NW, 1) + w)
                    nc.vector.tensor_scalar(rel[:, a.par, :], rel[:, a.par, :], -float(WINDOW), None,
                                            ALU.add).then_inc(rel_moved, 1)
                    dve.wait_ge(scat_mm, a.n(NW, 1) + w)
                    add_window(w * WINDOW).then_inc(acc_done, 1)

            def program(is_general):
                def body(at, i):
                    one, two, three, four = (stage(at, by, i) for by in (1, 0, -1, -2))
                    if four is not None and is_general:
                        scatter(four, is_general)
                    if one is not None:
                        lengths(one)
                    if two is not None:
                        directions(two)
                        products1(two)
                    if one is not None:
                        split(one)
                    if two is not None:
                        sv_sum(two)
                    if four is not None and not is_general:
                        scatter(four, is_general)
                    if two is not None:
                        destinations(two, is_general)
                        destinations_kept(two)
                    if one is not None:
                        split_again(one)
                    if two is not None and not is_general:
                        dve.wait_ge(rel_done, two.n(1, 1))
                        wait(dve, scat_mm, two.n(1, -1))
                        one_hot(two.par).then_inc(hot_done, 1)
                    if three is not None:
                        products2(three)
                        sums2(three)
                    if two is not None:
                        between(two)
                    if three is not None:
                        messages(three, NW if is_general else 1)
                periods(dve, body)

            with dve.If(flag == 0):
                program(False)
            with dve.If(flag != 0):
                program(True)

            after = [0]

            def then(ins):
                after[0] += 1
                ins.then_inc(post, 1)
                dve.wait_ge(post, after[0])

            then(nc.vector.memset(mean[:, :], 0.0))
            dve.wait_ge(turn_acc, 1)
            dve.wait_ge(xn_in, 32 if N > (N // NB) * NB else 16)
            banks = (pw[:, 0, 0, :], pw[:, 0, 1, :], pw[:, 1, 0, :], pw[:, 1, 1, :], ph[:, :], p1[:, :], p2[:, :])
            per = 512 // F
            for c in range(-(-NB // per)):
                n = min(per, NB - c * per)
                part = xn[:, c * per:c * per + n, :]
                ins = nc.vector.tensor_tensor(part, part, banks[c][:, 0:F * n].rearrange("p (b f) -> p b f", f=F), ALU.add)
            then(ins)
            then(nc.vector.tensor_reduce(mean[:, :], xn[:, :, :], AX.X, ALU.add))
            nc.vector.tensor_scalar(mean[:, :], mean[:, :], 1.0 / F, None, ALU.mult).then_inc(s_pre, 1)
            dve.wait_ge(s_pre, steps[0] + 1)
            then(nc.vector.tensor_tensor(xn[:, :, :], xn[:, :, :], mean[:, :].unsqueeze(2).broadcast_to([P, NB, F]),
                                         ALU.subtract))
            sq = prod_v[:, :, :, :, :].rearrange("p a b c d -> p (a b c d)")
            half = (NB * F) // 2
            flat = xn[:, :, :].rearrange("p b f -> p (b f)")
            width = G * 3 * 2 * C * C
            assert NB * F <= 2 * width
            for c in range(2):
                b0, b1 = c * ((NB + 1) // 2), min(NB, (c + 1) * ((NB + 1) // 2))
                view = sq[:, 0:(b1 - b0) * F].rearrange("p (b f) -> p b f", f=F)
                nc.vector.tensor_tensor(view, xn[:, b0:b1, :], xn[:, b0:b1, :], ALU.mult).then_inc(s_pre, 1)
                dve.wait_ge(s_pre, steps[0] + 2 + 2 * c)
                nc.vector.tensor_reduce(var[:, b0:b1], view, AX.X, ALU.add).then_inc(s_pre, 1)
                dve.wait_ge(s_pre, steps[0] + 3 + 2 * c)
            then(nc.vector.tensor_scalar(var[:, :], var[:, :], 1.0 / F, EPS, ALU.mult, ALU.add))
            then(nc.vector.memset(mean[:, :], 0.0))
            dve.wait_ge(root_done, 1)
            then(nc.vector.reciprocal(mean[:, :], var[:, :]))
            then(nc.vector.tensor_tensor(xn[:, :, :], xn[:, :, :], mean[:, :].unsqueeze(2).broadcast_to([P, NB, F]),
                                         ALU.mult))
            then(nc.vector.memset(var[:, :], 0.0))


def kernel(x, src, dst, edge_attr_10, edge_attr_3, edge_weight,
           L0_gnn_fc1_w1, L0_gnn_fc1_w2, L0_gnn_fc2_w1, L0_gnn_fc2_w2):
    import numpy as np
    import concourse.bacc as bacc
    from concourse.bass_utils import run_bass_kernel_spmd

    nc = bacc.Bacc("TRN2", target_bir_lowering=False, num_devices=1)
    arrays = {
        "x": x, "src": src, "dst": dst, "emb_t": np.asarray(edge_attr_10).T, "vec": edge_attr_3, "weight": edge_weight,
        "fc1_w1": L0_gnn_fc1_w1, "fc1_w2": L0_gnn_fc1_w2, "fc2_w1": L0_gnn_fc2_w1, "fc2_w2": L0_gnn_fc2_w2,
    }
    arrays = {f"in_{k}": np.ascontiguousarray(v) for k, v in arrays.items()}
    args = [nc.dram_tensor(k, a.shape, mybir.dt.from_np(a.dtype), kind="ExternalInput").ap()
            for k, a in arrays.items()]
    args.append(nc.dram_tensor("out", arrays["in_x"].shape, F32, kind="ExternalOutput").ap())
    build_gnn_layer(nc, *args)
    result = run_bass_kernel_spmd(nc, [arrays], core_ids=[0])
    return result.results[0]["out"]
```

```python
from contextlib import ExitStack

import concourse.bass as bass
from concourse import mybir

P = 128
G = 8
SUPER = P * G
WINDOW = 64
C = 8
F = 32
H = 16
L1, L2 = 512, 384
PIECES = 6
KH = PIECES * H
EPS = 1e-5

ALU = mybir.AluOpType
ACT = mybir.ActivationFunctionType
AX = mybir.AxisListType
F32 = mybir.dt.float32
BF16 = mybir.dt.bfloat16
I32 = mybir.dt.int32
RMAX = bass.bass_isa.ReduceOp.max


def build_gnn_layer(nc, x, src, dst, emb_t, vec, weight, fc1_w1, fc1_w2, fc2_w1, fc2_w2, out):
    N = x.shape[0]
    E = src.shape[0]
    K1 = emb_t.shape[0]
    FULL = E // SUPER
    NS = FULL + (1 if E % SUPER else 0)
    REPEATED = NS * SUPER - E
    NB = -(-N // P)
    NW = -(-N // WINDOW)
    ACC = max(NB * P, NW * WINDOW) + WINDOW
    SCAN = -(-FULL // P)
    assert FULL >= 8 and NS <= 512 and SCAN * SUPER + SUPER <= ACC

    c1 = 1.0 / (4.0 * 32.0 ** 0.5)
    c2 = 1.0 / (4.0 * 4.0)
    r3 = 3.0 ** 0.5

    def rows(ap, width):
        flat = ap[0:FULL * SUPER] if width == 1 else ap[0:FULL * SUPER, :]
        pat = "(s p t) -> s p t" if width == 1 else "(s p t) k -> s p (t k)"
        return flat.rearrange(pat, p=P, t=G)

    def last_rows(ap, width):
        flat = ap[E - SUPER:E] if width == 1 else ap[E - SUPER:E, :]
        pat = "(p t) -> p t" if width == 1 else "(p t) k -> p (t k)"
        return flat.rearrange(pat, t=G)

    src_rows, dst_rows, wgt_rows, vec_rows = rows(src, 1), rows(dst, 1), rows(weight, 1), rows(vec, 3)
    emb_cols = emb_t[:, 0:FULL * SUPER].rearrange("k (s e) -> s k e", e=SUPER)

    with ExitStack() as ctx:
        def sb(name, shape, dt=F32):
            return ctx.enter_context(nc.sbuf_tensor(name, shape, dt))

        def sem(name):
            return ctx.enter_context(nc.semaphore(name))

        identity = sb("identity", [P, P])
        identity_bf = sb("identity_bf", [P, P], BF16)
        node_iota_i = sb("node_iota_i", [P, WINDOW], I32)
        node_iota = sb("node_iota", [P, WINDOW])
        edge_iota_i = sb("edge_iota_i", [P, G], I32)
        fresh = sb("fresh", [P, G])
        minus_half = sb("minus_half", [P, G])
        ones_row = sb("ones_row", [1, P])
        w1 = sb("w1", [K1, 2 * H])
        w2 = sb("w2", [H, L1 + L2])
        w2_rest = sb("w2_rest", [H, L1 + L2])
        w2_parts = sb("w2_parts", [H, 3, L1 + L2], BF16)
        w2_stack = sb("w2_stack", [KH, L1 + L2], BF16)
        base_i = sb("base_i", [1, NS], I32)
        base_row = sb("base_row", [1, NS])
        base = sb("base", [P, NS])
        span = sb("span", [P, 3, SCAN + 1])
        excess = sb("excess", [P, SCAN + 1])
        excess_low = sb("excess_low", [P, SCAN + 1])
        excess_one = sb("excess_one", [P, 1])
        excess_all = sb("excess_all", [P, 1])
        general = sb("general", [P, 1], I32)

        idx = sb("idx", [P, 2, 2, G], I32)
        emb = sb("emb", [K1, 2, SUPER])
        vecs = sb("vecs", [P, 2, G, 3])
        late = sb("late", [P, 2, G])
        late_dst = sb("late_dst", [P, 2, G], I32)
        nodes = sb("nodes", [P, 2, G, 2, F])
        norm2 = sb("norm2", [P, G])
        vsq = sb("vsq", [P, G, 3])
        inv = sb("inv", [P, G])
        r = sb("r", [P, 2, G, 3])
        S = sb("S", [P, 2, G, 4 * C])
        V = sb("V", [P, 2, G, 3, 2 * C])
        vr = sb("vr", [P, G, 3, 2 * C])
        hid = sb("hid", [P, 2 * G, H])
        hid_rest = sb("hid_rest", [P, 2 * G, H])
        hid_parts = sb("hid_parts", [P, 2, 2 * G, KH], BF16)
        hid_t = sb("hid_t", [KH, 3, G, P], BF16)
        wa = sb("wa", [P, G, L1])
        wb = sb("wb", [P, G, L2])
        prod_s = sb("prod_s", [P, G, 4 * C, C])
        prod_v = sb("prod_v", [P, G, 3, 2 * C, C])
        sv = sb("sv", [P, G, C])
        M = sb("M", [P, G, 2 * C])
        VT = sb("VT", [P, G, 3, C])
        vtr = sb("vtr", [P, G, 3, C])
        prod_g = sb("prod_g", [P, G, 2, 2 * C, C])
        prod_o = sb("prod_o", [P, G, 4, C, C])
        osum = sb("osum", [P, G, 4, C])
        th = sb("th", [P, G, 2, C])
        gate = sb("gate", [P, G, C])
        q = sb("q", [P, G, 3, C])
        msg = sb("msg", [P, G, F])
        rel = sb("rel", [P, 2, G])
        rel_raw = sb("rel_raw", [P, G])
        hot = sb("hot", [P, 2, G, WINDOW])
        acc = sb("acc", [P, ACC])

        xn = sb("xn", [P, NB, F])
        mean = sb("mean", [P, NB])
        var = sb("var", [P, NB])

        pw = ctx.enter_context(nc.psum_tensor("pw", [P, 2, 2, 512], F32))
        pt = ctx.enter_context(nc.psum_tensor("pt", [KH, G, P], BF16))
        ph = ctx.enter_context(nc.psum_tensor("ph", [P, 512], F32))
        p1 = ctx.enter_context(nc.psum_tensor("p1", [P, 512], F32))
        p2 = ctx.enter_context(nc.psum_tensor("p2", [P, 512], F32))
        hid_ps = ph[:, 0:G * 2 * H].rearrange("p (t h) -> p t h", h=2 * H)
        vs_ps = p1[:, 0:G * 3 * C].rearrange("p (t k w) -> p t k w", k=3, w=C)
        st_ps = p1[:, G * 3 * C:G * 4 * C].rearrange("p (t w) -> p t w", w=C)
        gates_ps = p2[:, 0:G * 2 * C].rearrange("p (t a w) -> p t a w", a=2, w=C)
        scat_ps = ph[0:F, G * 2 * H:G * 2 * H + WINDOW]

        s_const = sem("s_const")
        s_w_in = sem("s_w_in")
        s_base_in = sem("s_base_in")
        s_scan_in = sem("s_scan_in")
        s_pre = sem("s_pre")
        s_parts = sem("s_parts")
        s_stack = sem("s_stack")
        s_base_row = sem("s_base_row")
        s_base_ps = sem("s_base_ps")
        s_excess = sem("s_excess")
        s_excess_all = sem("s_excess_all")
        s_general = sem("s_general")
        idx_in = [sem(f"idx_in{i}") for i in range(2)]
        emb_in = [sem(f"emb_in{i}") for i in range(2)]
        vec_in = [sem(f"vec_in{i}") for i in range(2)]
        wgt_in = [sem(f"wgt_in{i}") for i in range(2)]
        late_in = [sem(f"late_in{i}") for i in range(2)]
        nodes_in = [[sem(f"nodes_in{i}{k}") for k in range(2)] for i in range(2)]
        vsq_done = sem("vsq_done")
        norm2_done = sem("norm2_done")
        inv_done = sem("inv_done")
        r_done = sem("r_done")
        sv_copied = sem("sv_copied")
        vr_done = sem("vr_done")
        vdot_done = sem("vdot_done")
        hid_mm = sem("hid_mm")
        hid_done = sem("hid_done")
        hid_a = sem("hid_a")
        hid_b = sem("hid_b")
        hid_rest_done = sem("hid_rest_done")
        hid_c = sem("hid_c")
        turned = sem("turned")
        turned_out = sem("turned_out")
        wa_mm = sem("wa_mm")
        wa_out = sem("wa_out")
        wb_mm = sem("wb_mm")
        wb_out = sem("wb_out")
        pv_done = sem("pv_done")
        ps_done = sem("ps_done")
        p2_done = sem("p2_done")
        sv_done = sem("sv_done")
        vs_sum = sem("vs_sum")
        st_sum = sem("st_sum")
        m_st = sem("m_st")
        vt_part = sem("vt_part")
        vt_done = sem("vt_done")
        vtr_done = sem("vtr_done")
        m_vd = sem("m_vd")
        pg_done = sem("pg_done")
        po_done = sem("po_done")
        osum_done = sem("osum_done")
        gates_sum = sem("gates_sum")
        tanh_done = sem("tanh_done")
        gate_done = sem("gate_done")
        q_done = sem("q_done")
        msg_done = sem("msg_done")
        rel_raw_done = sem("rel_raw_done")
        rel_done = sem("rel_done")
        hot_done = sem("hot_done")
        scat_mm = sem("scat_mm")
        acc_done = sem("acc_done")
        rel_kept = sem("rel_kept")
        rel_moved = sem("rel_moved")
        gathers_begun = sem("gathers_begun")
        windows_begun_pe = sem("windows_begun_pe")
        windows_begun_dve = sem("windows_begun_dve")
        xn_in = sem("xn_in")
        turn_acc = sem("turn_acc")
        post = sem("post")
        root_done = sem("root_done")
        out_done = sem("out_done")

        class At:

            def __init__(self, b, d):
                self.b, self.par, self.half = b, d % 2, b + d // 2
                self.static = isinstance(b, int)
                self.d = d

            def n(self, per=1, more=0):
                return self.b * (2 * per) + (self.d * per + more)

            def k(self, per, more=0):
                return self.b * per + (per * (self.d // 2 + 1) + more)

            def before(self, by):
                return At(self.b, self.d - by)

            def index(self):
                return self.b * 2 + self.d

            def is_last(self):
                return self.static and 2 * self.b + self.d == NS - 1 and NS != FULL

        def wait(eng, semaphore, value):
            if isinstance(value, int) and value <= 0:
                return
            eng.wait_ge(semaphore, value)

        def periods(eng, body):
            first = 4
            pairs = (FULL - 3 - first) // 2
            for i in range(-2, first):
                body(At(0, i), i)
            with eng.Fori(0, pairs) as b:
                body(At(b + first // 2, 0), None)
                body(At(b + first // 2, 1), None)
            for i in range(first + 2 * pairs, NS + 2):
                body(At(i // 2, i % 2), i)

        def stage(at, by, i):
            if i is not None and not 0 <= i + by < NS:
                return None
            return At(at.b, at.d + by)

        block = ctx.enter_context(nc.Block())

        @block.sync
        def _(sp):
            sp.dma_start(base_i[0:1, 0:FULL], dst[0:FULL * SUPER].rearrange("(a s e) -> a s e", a=1, e=SUPER)[:, :, 0],
                         allow_slow_non_contiguous=True).then_inc(s_base_in, 16)
            if NS != FULL:
                sp.dma_start(base_i[0:1, FULL:NS], dst[E - SUPER:E - SUPER + 1].rearrange("(a s) -> a s", a=1)
                             ).then_inc(s_base_in, 16)
            scan = acc[:, :].bitcast(I32)
            for c in range(SCAN):
                n = min(P, FULL - c * P)
                sp.dma_start(scan[0:n, c * SUPER:(c + 1) * SUPER],
                             dst[c * P * SUPER:(c * P + n) * SUPER].rearrange("(s e) -> s e", e=SUPER)
                             ).then_inc(s_scan_in, 16)
            sp.dma_start(scan[0:1, SCAN * SUPER:(SCAN + 1) * SUPER],
                         dst[E - SUPER:E].rearrange("(a e) -> a e", a=1)).then_inc(s_scan_in, 16)
            sp.dma_start(w1[:, 0:H], fc1_w1).then_inc(s_w_in, 16)
            sp.dma_start(w1[:, H:2 * H], fc2_w1).then_inc(s_w_in, 16)
            sp.dma_start(w2[:, 0:L1], fc1_w2).then_inc(s_w_in, 16)
            sp.dma_start(w2[:, L1:L1 + L2], fc2_w2).then_inc(s_w_in, 16)

            def load_early(a):
                p, s, two, last = a.par, a.index(), a.before(2), a.is_last()
                for k in range(2):
                    wait(sp, nodes_in[p][k], two.k(16 * G))
                sp.dma_start(idx[:, p, 0, :], last_rows(src, 1) if last else src_rows[s]).then_inc(idx_in[p], 16)
                sp.dma_start(idx[:, p, 1, :], last_rows(dst, 1) if last else dst_rows[s]).then_inc(idx_in[p], 16)
                wait(sp, hid_mm, two.n(1, 1))
                sp.dma_start(emb[:, p, :], emb_t[:, E - SUPER:E] if last else emb_cols[s]).then_inc(emb_in[p], 16)

            def load_vectors(a):
                p, s, two, last = a.par, a.index(), a.before(2), a.is_last()
                wait(sp, r_done, two.n(1, 1))
                sp.dma_start(vecs[:, p, :, :].rearrange("p t k -> p (t k)"),
                             last_rows(vec, 3) if last else vec_rows[s]).then_inc(vec_in[p], 16)

            def load_weights(a):
                p, s, two, last = a.par, a.index(), a.before(2), a.is_last()
                wait(sp, msg_done, two.n(2, 2))
                sp.dma_start(late[:, p, :], last_rows(weight, 1) if last else wgt_rows[s]).then_inc(wgt_in[p], 16)

            def load_destinations(a):
                p, s, two, last = a.par, a.index(), a.before(2), a.is_last()
                wait(sp, rel_raw_done, two.n(1, 1))
                sp.dma_start(late_dst[:, p, :], last_rows(dst, 1) if last else dst_rows[s]).then_inc(late_in[p], 16)

            load_early(At(0, 0))
            sp.wait_ge(s_parts, 1)
            for g, part in enumerate((0, 1, 2, 0, 1, 0)):
                sp.dma_start(w2_stack[H * g:H * g + H, :], w2_parts[:, part, :]).then_inc(s_stack, 16)

            def body(at, i):
                for load, ahead in ((load_early, 3), (load_vectors, 2), (load_destinations, 1), (load_weights, 0)):
                    a = stage(at, ahead, i)
                    if a is not None:
                        load(a)

            periods(sp, body)
            whole = N // NB
            sp.dma_start(xn[0:whole, :, :].rearrange("p b f -> p (b f)"),
                         x[0:whole * NB, :].rearrange("(p b) f -> p (b f)", b=NB)).then_inc(xn_in, 16)
            if N > whole * NB:
                sp.dma_start(xn[whole:whole + 1, 0:N - whole * NB, :].rearrange("p b f -> p (b f)"),
                             x[whole * NB:N, :].rearrange("(p b) f -> p (b f)", p=1)).then_inc(xn_in, 16)
            sp.wait_ge(post, 9)
            sp.dma_start(out[0:whole * NB, :].rearrange("(p b) f -> p (b f)", b=NB),
                         xn[0:whole, :, :].rearrange("p b f -> p (b f)")).then_inc(out_done, 16)
            if N > whole * NB:
                sp.dma_start(out[whole * NB:N, :].rearrange("(p b) f -> p (b f)", p=1),
                             xn[whole:whole + 1, 0:N - whole * NB, :].rearrange("p b f -> p (b f)")
                             ).then_inc(out_done, 16)
            sp.wait_ge(out_done, 32 if N > whole * NB else 16)

        @block.gpsimd
        def _(pool):
            nc.gpsimd.memset(identity[:, :], 0.0).then_inc(s_const, 1)
            nc.gpsimd.memset(identity_bf[:, :], 0.0).then_inc(s_const, 1)
            nc.gpsimd.memset(minus_half[:, :], -0.5).then_inc(s_const, 1)
            nc.gpsimd.memset(ones_row[:, :], 1.0).then_inc(s_const, 1)
            nc.gpsimd.iota(node_iota_i[:, :], pattern=[[1, WINDOW]], base=0, channel_multiplier=0).then_inc(s_const, 1)
            nc.gpsimd.iota(edge_iota_i[:, :], pattern=[[1, G]], base=0, channel_multiplier=G).then_inc(s_const, 1)
            nc.gpsimd.memset(xn[:, :, :], 0.0).then_inc(s_const, 1)
            pool.wait_ge(s_const, 7)
            for m in (identity, identity_bf):
                nc.gpsimd.affine_select(out=m[:, :], in_=m[:, :], compare_op=ALU.not_equal, fill=1.0, base=0,
                                        pattern=[[-1, P]], channel_multiplier=1).then_inc(s_const, 1)

            def gathers(a):
                p = a.par
                pool.wait_ge(idx_in[p], a.k(32))
                wait(pool, sv_copied, a.before(2).n(4, 4))
                pool.sem_inc(gathers_begun, 1)
                for side in range(2):
                    for t in range(G):
                        nc.gpsimd.indirect_dma_start(
                            nodes[:, p, t, side, :], None, x,
                            bass.IndirectOffsetOnAxis(ap=idx[:, p, side, t:t + 1], axis=0)
                        ).then_inc(nodes_in[p][side], 16)

            def inverse(a):
                pool.wait_ge(norm2_done, a.n(1, 1))
                wait(pool, r_done, a.n())
                nc.gpsimd.tensor_tensor(inv[:, :], norm2[:, :], minus_half[:, :], ALU.pow).then_inc(inv_done, 1)

            pool.wait_ge(s_excess, 1)
            nc.gpsimd.partition_all_reduce(excess_all[:, :], excess_one[:, :], P, RMAX).then_inc(s_excess_all, 1)

            def body(at, i):
                a = stage(at, 1, i)
                if a is not None:
                    inverse(a)
                a = stage(at, 2, i)
                if a is not None:
                    gathers(a)

            periods(pool, body)

        @block.scalar
        def _(act):
            def rows_laid_out(a):
                p = a.par
                wait(act, p2_done, a.before(2).n(1, 1))
                for side in range(2):
                    act.wait_ge(nodes_in[p][side], a.k(16 * G))
                    c = slice(C * side, C * side + C)
                    nc.scalar.activation(S[:, p, :, c], nodes[:, p, :, side, 0:C], ACT.Copy).then_inc(sv_copied, 1)
                    nc.scalar.activation(V[:, p, :, :, c],
                                         nodes[:, p, :, side, C:F].rearrange("p t (u k) -> p t k u", k=3),
                                         ACT.Copy).then_inc(sv_copied, 1)

            def hidden_parts(a):
                act.wait_ge(hid_mm, a.n(1, 1))
                wait(act, hid_rest_done, a.n())
                nc.scalar.activation(hid[:, :, :].rearrange("p (t l) h -> p t (l h)", l=2), hid_ps, ACT.Relu,
                                     scale=float(K1) ** -0.5).then_inc(hid_done, 1)
                act.wait_ge(hid_done, a.n(1, 1))
                wait(act, turned, a.n(2, -2))
                parts = hid_parts[:, a.par, :, :].rearrange("p a (g h) -> p a g h", h=H)
                nc.scalar.activation(parts[:, :, 0:3, :], hid[:, :, :].unsqueeze(2).broadcast_to([P, 2 * G, 3, H]),
                                     ACT.Copy).then_inc(hid_a, 1)

            def hidden_second(a):
                parts = hid_parts[:, a.par, :, :].rearrange("p a (g h) -> p a g h", h=H)
                act.wait_ge(hid_rest_done, a.n(1, 1))
                nc.scalar.activation(parts[:, :, 3:5, :], hid_rest[:, :, :].unsqueeze(2).broadcast_to([P, 2 * G, 2, H]),
                                     ACT.Copy).then_inc(hid_b, 1)

            def turned_copy(a, layer):
                act.wait_ge(turned, a.n(2, layer + 1))
                wait(act, (wa_mm, wb_mm)[layer], a.n(4, -4 * layer))
                nc.scalar.activation(hid_t[:, layer and 1 + a.par, :, :], pt[:, :, :], ACT.Copy).then_inc(turned_out, 1)

            def weights_out(a, layer, pairs):
                buf, width, made, taken, used = ((wa, L1, wa_mm, wa_out, sv_done), (wb, L2, wb_mm, wb_out, osum_done))[layer]
                wait(act, used, a.n())
                for pair in pairs:
                    act.wait_ge(made, a.n(4, pair + 1))
                    nc.scalar.activation(buf[:, 2 * pair:2 * pair + 2, :], pw[:, pair % 2, :, 0:width],
                                         ACT.Copy).then_inc(taken, 1)

            def tanhs(a):
                act.wait_ge(gates_sum, a.n(1, 1))
                wait(act, msg_done, a.n(2))
                nc.scalar.activation(th[:, :, :, :], gates_ps, ACT.Tanh).then_inc(tanh_done, 1)

            def body(at, i):
                zero, one, three = stage(at, 2, i), stage(at, 1, i), stage(at, -1, i)
                if three is not None:
                    weights_out(three, 1, (0, 1))
                if one is not None:
                    turned_copy(one, 0)
                if three is not None:
                    weights_out(three, 1, (2, 3))
                if zero is not None:
                    hidden_parts(zero)
                    hidden_second(zero)
                if one is not None:
                    turned_copy(one, 1)
                    rows_laid_out(one)
                if one is not None:
                    weights_out(one, 0, (0, 1, 2, 3))
                if three is not None:
                    tanhs(three)

            periods(act, body)
            act.wait_ge(post, 6)
            nc.scalar.activation(var[:, :], var[:, :], ACT.Sqrt).then_inc(root_done, 1)

        @block.tensor
        def _(pe):
            pe.wait_ge(s_const, 9)
            pe.wait_ge(s_base_row, 1)
            nc.tensor.matmul(ph[:, 0:NS], ones_row[:, :], base_row[:, :], start=True, stop=True).then_inc(s_base_ps, 1)
            pe.wait_ge(s_general, 1)
            pe.wait_ge(s_w_in, 64)
            pe.wait_ge(s_stack, 16 * PIECES)
            flag = nc.tensor.value_load(general[0:1, 0:1], min_val=0, max_val=1)

            def hidden(a, windows, more):
                p = a.par
                pe.wait_ge(emb_in[p], a.k(16))
                wait(pe, hid_done, a.n())
                wait(pe, acc_done, a.n(windows, more - 4 * windows))
                for t in range(G):
                    mm = nc.tensor.matmul(hid_ps[:, t, :], emb[:, p, t:SUPER:G], w1[:, :], start=True, stop=True)
                mm.then_inc(hid_mm, 1)

            def turn(a, layer):
                pe.wait_ge(hid_a, a.n(1, 1))
                pe.wait_ge(hid_b, a.n(1, 1))
                pe.wait_ge(hid_c, a.n(1, 1))
                wait(pe, turned_out, a.n(2, layer))
                for t in range(G):
                    mm = nc.tensor.transpose(pt[:, t, :], hid_parts[:, a.par, 2 * t + layer, :], identity_bf[:, :])
                mm.then_inc(turned, 1)

            def edge_weights(a, layer, pairs, free):
                made, taken = ((wa_mm, wa_out), (wb_mm, wb_out))[layer]
                lo, width = ((0, L1), (L1, L2))[layer]
                pe.wait_ge(turned_out, a.n(2, layer + 1))
                for pair in pairs:
                    if pair == 0:
                        wait(pe, *free)
                    if pair >= 2:
                        pe.wait_ge(taken, a.n(4, pair - 1))
                    for t in range(2):
                        mm = nc.tensor.matmul(pw[:, pair % 2, t, 0:width], hid_t[:, layer and 1 + a.par, 2 * pair + t, :],
                                              w2_stack[:, lo:lo + width], start=True, stop=True)
                    mm.then_inc(made, 1)

            def vector_sums(a):
                pe.wait_ge(pv_done, a.n(1, 1))
                wait(pe, vt_done, a.n())
                wait(pe, m_st, a.n())
                for u in range(2 * C):
                    mm = nc.tensor.matmul(vs_ps, identity[:, :], prod_v[:, :, :, u, :],
                                          start=(u == 0), stop=(u == 2 * C - 1))
                mm.then_inc(vs_sum, 1)

            def scalar_sums(a):
                pe.wait_ge(ps_done, a.n(1, 1))
                for u in range(4 * C):
                    mm = nc.tensor.matmul(st_ps, identity[:, :], prod_s[:, :, u, :],
                                          start=(u == 0), stop=(u == 4 * C - 1))
                mm.then_inc(st_sum, 1)

            def gate_sums(a, half):
                if half == 0:
                    pe.wait_ge(pg_done, a.n(1, 1))
                    wait(pe, tanh_done, a.n())
                for u in range(C * half, C * half + C):
                    mm = nc.tensor.matmul(gates_ps, identity[:, :], prod_g[:, :, :, u, :],
                                          start=(u == 0), stop=(u == 2 * C - 1))
                if half == 1:
                    mm.then_inc(gates_sum, 1)

            def window(par):
                for t in range(G):
                    mm = nc.tensor.matmul(scat_ps, msg[:, t, :], hot[:, par, t, :], start=(t == 0), stop=(t == G - 1))
                mm.then_inc(scat_mm, 1)

            def scatter(a, is_general):
                pe.wait_ge(msg_done, a.n(2, 2))
                ahead = a.n(1, 5)
                pe.wait_ge(hid_done, min(ahead, NS) if a.static else ahead)
                if not is_general:
                    pe.wait_ge(hot_done, a.n(1, 1))
                    wait(pe, acc_done, a.n())
                    window(a.par)
                    return
                pe.sem_inc(windows_begun_pe, 1)
                with pe.Fori(0, NW) as w:
                    pe.wait_ge(hot_done, a.n(NW, 1) + w)
                    pe.wait_ge(acc_done, a.n(NW, 1) + w)
                    window(a.par)

            def program(is_general):
                def body(at, i):
                    zero, one, two, three, four = (stage(at, by, i) for by in (2, 1, 0, -1, -2))
                    if three is not None:
                        for_wb = (wa_out, three.n(4, 8) if two is not None else three.n(4, 4))
                        edge_weights(three, 1, (0, 1), for_wb)
                    if one is not None:
                        turn(one, 0)
                    if zero is not None:
                        hidden(zero, NW if is_general else 1, int(is_general))
                    if three is not None:
                        edge_weights(three, 1, (2, 3), for_wb)
                    if two is not None:
                        vector_sums(two)
                    if one is not None:
                        turn(one, 1)
                    if two is not None:
                        scalar_sums(two)
                    if four is not None:
                        scatter(four, is_general)
                    if one is not None:
                        for_wa = (wb_out, one.n(4, -4))
                        edge_weights(one, 0, (0, 1), for_wa)
                    if three is not None:
                        gate_sums(three, 0)
                    if one is not None:
                        edge_weights(one, 0, (2, 3), for_wa)
                    if three is not None:
                        gate_sums(three, 1)
                periods(pe, body)

            with pe.If(flag == 0):
                program(False)
            with pe.If(flag != 0):
                pe.sem_inc(scat_mm, 1)
                program(True)
            pe.wait_ge(post, 1)
            banks = (pw[:, 0, 0, :], pw[:, 0, 1, :], pw[:, 1, 0, :], pw[:, 1, 1, :], ph[:, :], p1[:, :], p2[:, :])
            per = 512 // F
            for b in range(NB):
                mm = nc.tensor.matmul(banks[b // per][:, F * (b % per):F * (b % per) + F],
                                      acc[0:F, b:b + NB * (P - 1) + 1:NB], identity[0:F, 0:F], start=True, stop=True)
            mm.then_inc(turn_acc, 1)

        @block.vector
        def _(dve):
            steps = [0]

            def done(ins):
                steps[0] += 1
                ins.then_inc(s_pre, 1)
                dve.wait_ge(s_pre, steps[0])

            dve.wait_ge(s_w_in, 64)
            done(nc.vector.tensor_scalar(w2[:, 0:256], w2[:, 0:256], c1, None, ALU.mult))
            done(nc.vector.tensor_scalar(w2[:, 256:384], w2[:, 256:384], c1 * r3, None, ALU.mult))
            done(nc.vector.tensor_scalar(w2[:, 384:L1], w2[:, 384:L1], c1, None, ALU.mult))
            done(nc.vector.tensor_scalar(w2[:, L1:L1 + 256], w2[:, L1:L1 + 256], c2, None, ALU.mult))
            done(nc.vector.tensor_scalar(w2[:, L1 + 256:L1 + 320], w2[:, L1 + 256:L1 + 320], c2 * r3, None, ALU.mult))
            done(nc.vector.tensor_scalar(w2[:, L1 + 320:L1 + L2], w2[:, L1 + 320:L1 + L2], c2, None, ALU.mult))
            done(nc.vector.tensor_copy(w2_parts[:, 0, :], w2[:, :]))
            done(nc.vector.tensor_tensor(w2_rest[:, :], w2[:, :], w2_parts[:, 0, :], ALU.subtract))
            done(nc.vector.tensor_copy(w2_parts[:, 1, :], w2_rest[:, :]))
            nc.vector.tensor_tensor(w2_parts[:, 2, :], w2_rest[:, :], w2_parts[:, 1, :],
                                    ALU.subtract).then_inc(s_parts, 1)
            dve.wait_ge(s_base_in, 32 if NS != FULL else 16)
            nc.vector.tensor_copy(base_row[:, :], base_i[:, :]).then_inc(s_base_row, 1)
            done(nc.vector.memset(span[:, :, :], 0.0))
            dve.wait_ge(s_scan_in, 16 * (SCAN + 1))
            scan = acc[:, :].bitcast(I32)
            for c in range(SCAN + 1):
                n = min(P, FULL - c * P) if c < SCAN else 1
                part = scan[0:n, c * SUPER:(c + 1) * SUPER]
                done(nc.vector.tensor_reduce(span[0:n, 0, c:c + 1], part, AX.X, ALU.max))
                done(nc.vector.tensor_reduce(span[0:n, 1, c:c + 1], part, AX.X, ALU.min))
                done(nc.vector.tensor_copy(span[0:n, 2, c:c + 1], part[:, 0:1]))
            done(nc.vector.tensor_tensor(excess[:, :], span[:, 0, :], span[:, 2, :], ALU.subtract))
            done(nc.vector.tensor_scalar(excess[:, :], excess[:, :], -(WINDOW - 1.0), None, ALU.add))
            done(nc.vector.tensor_tensor(excess_low[:, :], span[:, 2, :], span[:, 1, :], ALU.subtract))
            done(nc.vector.tensor_tensor(excess[:, :], excess[:, :], excess_low[:, :], ALU.max))
            nc.vector.tensor_reduce(excess_one[:, :], excess[:, :], AX.X, ALU.max).then_inc(s_excess, 1)
            done(nc.vector.memset(acc[:, :], 0.0))
            dve.wait_ge(s_const, 9)
            done(nc.vector.tensor_copy(node_iota[:, :], node_iota_i[:, :]))
            done(nc.vector.tensor_scalar(fresh[:, :], edge_iota_i[:, :], float(REPEATED), None, ALU.is_ge))
            dve.wait_ge(s_base_ps, 1)
            done(nc.vector.tensor_copy(base[:, :], ph[:, 0:NS]))
            dve.wait_ge(s_excess_all, 1)
            nc.vector.tensor_scalar(general[:, :], excess_all[:, :], 0.0, None, ALU.is_gt).then_inc(s_general, 1)
            dve.wait_ge(s_general, 1)
            flag = nc.vector.value_load(general[0:1, 0:1], min_val=0, max_val=1)

            def lengths(a):
                p = a.par
                dve.wait_ge(vec_in[p], a.k(16))
                nc.vector.tensor_tensor(vsq[:, :, :], vecs[:, p, :, :], vecs[:, p, :, :], ALU.mult).then_inc(vsq_done, 1)
                dve.wait_ge(vsq_done, a.n(1, 1))
                wait(dve, inv_done, a.n())
                nc.vector.tensor_reduce(norm2[:, :], vsq[:, :, :], AX.X, ALU.add).then_inc(norm2_done, 1)

            def split(a):
                dve.wait_ge(hid_a, a.n(1, 1))
                wait(dve, hid_b, a.n())
                nc.vector.tensor_tensor(hid_rest[:, :, :], hid[:, :, :], hid_parts[:, a.par, :, 0:H],
                                        ALU.subtract).then_inc(hid_rest_done, 1)

            def split_again(a):
                dve.wait_ge(hid_b, a.n(1, 1))
                nc.vector.tensor_tensor(hid_parts[:, a.par, :, KH - H:KH], hid_rest[:, :, :], hid_parts[:, a.par, :, 3 * H:4 * H],
                                        ALU.subtract).then_inc(hid_c, 1)

            def directions(a):
                p = a.par
                dve.wait_ge(inv_done, a.n(1, 1))
                dve.wait_ge(vec_in[p], a.k(16))
                nc.vector.tensor_tensor(r[:, p, :, :], vecs[:, p, :, :],
                                        inv[:, :].unsqueeze(2).broadcast_to([P, G, 3]), ALU.mult).then_inc(r_done, 1)
                dve.wait_ge(r_done, a.n(1, 1))
                dve.wait_ge(sv_copied, a.n(4, 4))
                nc.vector.tensor_tensor(vr[:, :, :, :], V[:, p, :, :, :],
                                        r[:, p, :, :].unsqueeze(3).broadcast_to([P, G, 3, 2 * C]),
                                        ALU.mult).then_inc(vr_done, 1)

            def vdots(a):
                dve.wait_ge(vr_done, a.n(1, 1))
                nc.vector.tensor_reduce(S[:, a.par, :, 2 * C:4 * C], vr[:, :, :, :].rearrange("p t k u -> p t u k"),
                                        AX.X, ALU.add).then_inc(vdot_done, 1)

            def products1(a):
                p = a.par
                dve.wait_ge(wa_out, a.n(4, 4))
                wait(dve, vs_sum, a.n())
                nc.vector.tensor_tensor(
                    prod_v[:, :, :, :, :],
                    wa[:, :, 384:L1].rearrange("p t (u w) -> p t u w", w=C).unsqueeze(2).broadcast_to([P, G, 3, 2 * C, C]),
                    V[:, p, :, :, :].unsqueeze(4).broadcast_to([P, G, 3, 2 * C, C]), ALU.mult).then_inc(pv_done, 1)
                vdots(a)
                dve.wait_ge(vdot_done, a.n(1, 1))
                wait(dve, st_sum, a.n())
                nc.vector.tensor_tensor(
                    prod_s[:, :, :, :], wa[:, :, 0:256].rearrange("p t (u w) -> p t u w", w=C),
                    S[:, p, :, :].unsqueeze(3).broadcast_to([P, G, 4 * C, C]), ALU.mult).then_inc(ps_done, 1)
                third = wa[:, :, 256:384].rearrange("p t (u w) -> p t u w", w=C)
                nc.vector.tensor_tensor(
                    third, third, S[:, p, :, 0:2 * C].unsqueeze(3).broadcast_to([P, G, 2 * C, C]),
                    ALU.mult).then_inc(p2_done, 1)

            def sv_sum(a):
                dve.wait_ge(p2_done, a.n(1, 1))
                nc.vector.tensor_reduce(sv[:, :, :], wa[:, :, 256:384].rearrange("p t (u w) -> p t w u", w=C),
                                        AX.X, ALU.add).then_inc(sv_done, 1)

            def destinations(a, is_general):
                p = a.par
                dve.wait_ge(late_in[p], a.k(16))
                first = 0.0 if is_general else base[:, bass.ds(a.index(), 1)] if not a.static else base[:, a.index():a.index() + 1]
                nc.vector.tensor_scalar(rel_raw[:, :], late_dst[:, p, :], first, None, ALU.subtract).then_inc(rel_raw_done, 1)
                dve.wait_ge(rel_raw_done, a.n(1, 1))

            def destinations_kept(a):
                p = a.par
                if a.is_last():
                    nc.vector.scalar_tensor_tensor(rel[:, p, :], rel_raw[:, :], 1.0, fresh[:, :], ALU.add,
                                                   ALU.mult).then_inc(rel_kept, 1)
                    dve.wait_ge(rel_kept, 1)
                    nc.vector.tensor_scalar(rel[:, p, :], rel[:, p, :], -1.0, None, ALU.add).then_inc(rel_done, 1)
                else:
                    nc.vector.tensor_copy(rel[:, p, :], rel_raw[:, :]).then_inc(rel_done, 1)

            def one_hot(par):
                return nc.vector.tensor_tensor(
                    hot[:, par, :, :], node_iota[:, :].unsqueeze(1).broadcast_to([P, G, WINDOW]),
                    rel[:, par, :].unsqueeze(2).broadcast_to([P, G, WINDOW]), ALU.is_equal)

            def products2(a):
                dve.wait_ge(wb_out, a.n(4, 4))
                dve.wait_ge(m_st, a.n(1, 1))
                dve.wait_ge(m_vd, a.n(1, 1))
                wait(dve, gates_sum, a.n())
                for half in range(2):
                    ins = nc.vector.tensor_tensor(
                        prod_g[:, :, half, :, :],
                        wb[:, :, 128 * half:128 * half + 128].rearrange("p t (u w) -> p t u w", w=C),
                        M[:, :, :].unsqueeze(3).broadcast_to([P, G, 2 * C, C]), ALU.mult)
                ins.then_inc(pg_done, 1)
                nc.vector.tensor_tensor(
                    prod_o[:, :, 0:3, :, :],
                    wb[:, :, 320:L2].rearrange("p t (u w) -> p t u w", w=C).unsqueeze(2).broadcast_to([P, G, 3, C, C]),
                    VT[:, :, :, :].unsqueeze(4).broadcast_to([P, G, 3, C, C]), ALU.mult).then_inc(po_done, 1)
                nc.vector.tensor_tensor(
                    prod_o[:, :, 3, :, :], wb[:, :, 256:320].rearrange("p t (u w) -> p t u w", w=C),
                    M[:, :, 0:C].unsqueeze(3).broadcast_to([P, G, C, C]), ALU.mult).then_inc(po_done, 1)

            def sums2(a):
                dve.wait_ge(po_done, a.n(2, 2))
                nc.vector.tensor_reduce(
                    osum[:, :, :, :].rearrange("p t k w -> p (t k) w"),
                    prod_o[:, :, :, :, :].rearrange("p t k u w -> p (t k) w u"), AX.X, ALU.add).then_inc(osum_done, 1)

            def between(a):
                p = a.par
                rb = r[:, p, :, :].unsqueeze(3).broadcast_to([P, G, 3, C])
                dve.wait_ge(sv_done, a.n(1, 1))
                wait(dve, po_done, a.n(2))
                nc.vector.tensor_tensor(VT[:, :, :, :], sv[:, :, :].unsqueeze(2).broadcast_to([P, G, 3, C]), rb,
                                        ALU.mult).then_inc(vt_part, 1)
                dve.wait_ge(vs_sum, a.n(1, 1))
                dve.wait_ge(st_sum, a.n(1, 1))
                dve.wait_ge(vt_part, a.n(1, 1))
                nc.vector.tensor_tensor(VT[:, :, :, :], VT[:, :, :, :], vs_ps, ALU.add).then_inc(vt_done, 1)
                dve.wait_ge(vt_done, a.n(1, 1))
                nc.vector.tensor_tensor(vtr[:, :, :, :], VT[:, :, :, :], rb, ALU.mult).then_inc(vtr_done, 1)
                nc.vector.tensor_copy(M[:, :, 0:C], st_ps).then_inc(m_st, 1)
                dve.wait_ge(vtr_done, a.n(1, 1))
                nc.vector.tensor_reduce(M[:, :, C:2 * C], vtr[:, :, :, :].rearrange("p t k w -> p t w k"), AX.X,
                                        ALU.add).then_inc(m_vd, 1)

            def vectors_out(a):
                rb = r[:, a.par, :, :].unsqueeze(3).broadcast_to([P, G, 3, C])
                dve.wait_ge(osum_done, a.n(1, 1))
                wait(dve, msg_done, a.n(2))
                nc.vector.tensor_tensor(q[:, :, :, :], osum[:, :, 3, :].unsqueeze(2).broadcast_to([P, G, 3, C]), rb,
                                        ALU.mult).then_inc(q_done, 1)
                dve.wait_ge(q_done, a.n(2, 1))
                nc.vector.tensor_tensor(q[:, :, :, :], q[:, :, :, :], osum[:, :, 0:3, :], ALU.add).then_inc(q_done, 1)

            def messages(a, windows, more):
                p = a.par
                weights = late[:, p, :].unsqueeze(2).broadcast_to([P, G, C])
                dve.wait_ge(wgt_in[p], a.k(16))
                dve.wait_ge(tanh_done, a.n(1, 1))
                nc.vector.tensor_tensor(gate[:, :, :], th[:, :, 1, :], weights, ALU.mult).then_inc(gate_done, 1)
                wait(dve, scat_mm, a.n(windows, more))
                nc.vector.tensor_tensor(msg[:, :, 0:C], th[:, :, 0, :], weights, ALU.mult).then_inc(msg_done, 1)
                dve.wait_ge(q_done, a.n(2, 2))
                dve.wait_ge(gate_done, a.n(1, 1))
                nc.vector.tensor_tensor(
                    msg[:, :, C:F].rearrange("p t (w k) -> p t k w", k=3), q[:, :, :, :],
                    gate[:, :, :].unsqueeze(2).broadcast_to([P, G, 3, C]), ALU.mult).then_inc(msg_done, 1)

            def add_window(first):
                cols = acc[0:F, bass.ds(first, WINDOW)]
                return nc.vector.tensor_tensor(cols, cols, scat_ps, ALU.add)

            def scatter(a, is_general):
                if not is_general:
                    dve.wait_ge(scat_mm, a.n(1, 1))
                    wait(dve, acc_done, a.n())
                    first = nc.vector.value_load(base_i[0:1, bass.ds(a.index(), 1)], min_val=0, max_val=N - 1)
                    add_window(first).then_inc(acc_done, 1)
                    return
                dve.wait_ge(rel_done, a.n(1, 1))
                dve.sem_inc(windows_begun_dve, 1)
                with dve.Fori(0, NW) as w:
                    dve.wait_ge(scat_mm, a.n(NW, 1) + w)
                    dve.wait_ge(rel_moved, a.n(NW, 1) + w)
                    one_hot(a.par).then_inc(hot_done, 1)
                    dve.wait_ge(hot_done, a.n(NW, 1) + w)
                    nc.vector.tensor_scalar(rel[:, a.par, :], rel[:, a.par, :], -float(WINDOW), None,
                                            ALU.add).then_inc(rel_moved, 1)
                    dve.wait_ge(scat_mm, a.n(NW, 2) + w)
                    add_window(w * WINDOW).then_inc(acc_done, 1)

            def program(is_general):
                def body(at, i):
                    zero, one, two, three, four = (stage(at, by, i) for by in (2, 1, 0, -1, -2))
                    windows = NW if is_general else 1
                    if one is not None:
                        lengths(one)
                    if two is not None:
                        directions(two)
                        products1(two)
                    if zero is not None:
                        split(zero)
                    if two is not None:
                        sv_sum(two)
                    if four is not None:
                        messages(four, windows, int(is_general))
                        if is_general:
                            scatter(four, is_general)
                    if two is not None:
                        destinations(two, is_general)
                        destinations_kept(two)
                    if three is not None:
                        products2(three)
                        sums2(three)
                        vectors_out(three)
                    if zero is not None:
                        split_again(zero)
                    if two is not None:
                        between(two)
                    if four is not None and not is_general:
                        scatter(four, is_general)
                    if two is not None and not is_general:
                        dve.wait_ge(rel_done, two.n(1, 1))
                        wait(dve, scat_mm, two.n(1, -1))
                        one_hot(two.par).then_inc(hot_done, 1)
                periods(dve, body)

            with dve.If(flag == 0):
                program(False)
            with dve.If(flag != 0):
                dve.sem_inc(acc_done, 1)
                dve.sem_inc(rel_moved, 1)
                program(True)

            after = [0]

            def then(ins):
                after[0] += 1
                ins.then_inc(post, 1)
                dve.wait_ge(post, after[0])

            then(nc.vector.memset(mean[:, :], 0.0))
            dve.wait_ge(turn_acc, 1)
            dve.wait_ge(xn_in, 32 if N > (N // NB) * NB else 16)
            banks = (pw[:, 0, 0, :], pw[:, 0, 1, :], pw[:, 1, 0, :], pw[:, 1, 1, :], ph[:, :], p1[:, :], p2[:, :])
            per = 512 // F
            for c in range(-(-NB // per)):
                n = min(per, NB - c * per)
                part = xn[:, c * per:c * per + n, :]
                ins = nc.vector.tensor_tensor(part, part, banks[c][:, 0:F * n].rearrange("p (b f) -> p b f", f=F), ALU.add)
            then(ins)
            then(nc.vector.tensor_reduce(mean[:, :], xn[:, :, :], AX.X, ALU.add))
            nc.vector.tensor_scalar(mean[:, :], mean[:, :], 1.0 / F, None, ALU.mult).then_inc(s_pre, 1)
            dve.wait_ge(s_pre, steps[0] + 1)
            then(nc.vector.tensor_tensor(xn[:, :, :], xn[:, :, :], mean[:, :].unsqueeze(2).broadcast_to([P, NB, F]),
                                         ALU.subtract))
            sq = prod_v[:, :, :, :, :].rearrange("p a b c d -> p (a b c d)")
            half = (NB * F) // 2
            flat = xn[:, :, :].rearrange("p b f -> p (b f)")
            width = G * 3 * 2 * C * C
            assert NB * F <= 2 * width
            for c in range(2):
                b0, b1 = c * ((NB + 1) // 2), min(NB, (c + 1) * ((NB + 1) // 2))
                view = sq[:, 0:(b1 - b0) * F].rearrange("p (b f) -> p b f", f=F)
                nc.vector.tensor_tensor(view, xn[:, b0:b1, :], xn[:, b0:b1, :], ALU.mult).then_inc(s_pre, 1)
                dve.wait_ge(s_pre, steps[0] + 2 + 2 * c)
                nc.vector.tensor_reduce(var[:, b0:b1], view, AX.X, ALU.add).then_inc(s_pre, 1)
                dve.wait_ge(s_pre, steps[0] + 3 + 2 * c)
            then(nc.vector.tensor_scalar(var[:, :], var[:, :], 1.0 / F, EPS, ALU.mult, ALU.add))
            then(nc.vector.memset(mean[:, :], 0.0))
            dve.wait_ge(root_done, 1)
            then(nc.vector.reciprocal(mean[:, :], var[:, :]))
            then(nc.vector.tensor_tensor(xn[:, :, :], xn[:, :, :], mean[:, :].unsqueeze(2).broadcast_to([P, NB, F]),
                                         ALU.mult))
            then(nc.vector.memset(var[:, :], 0.0))


def kernel(x, src, dst, edge_attr_10, edge_attr_3, edge_weight,
           L0_gnn_fc1_w1, L0_gnn_fc1_w2, L0_gnn_fc2_w1, L0_gnn_fc2_w2):
    import numpy as np
    import concourse.bacc as bacc
    from concourse.bass_utils import run_bass_kernel_spmd

    nc = bacc.Bacc("TRN2", target_bir_lowering=False, num_devices=1)
    arrays = {
        "x": x, "src": src, "dst": dst, "emb_t": np.asarray(edge_attr_10).T, "vec": edge_attr_3, "weight": edge_weight,
        "fc1_w1": L0_gnn_fc1_w1, "fc1_w2": L0_gnn_fc1_w2, "fc2_w1": L0_gnn_fc2_w1, "fc2_w2": L0_gnn_fc2_w2,
    }
    arrays = {f"in_{k}": np.ascontiguousarray(v) for k, v in arrays.items()}
    args = [nc.dram_tensor(k, a.shape, mybir.dt.from_np(a.dtype), kind="ExternalInput").ap()
            for k, a in arrays.items()]
    args.append(nc.dram_tensor("out", arrays["in_x"].shape, F32, kind="ExternalOutput").ap())
    build_gnn_layer(nc, *args)
    result = run_bass_kernel_spmd(nc, [arrays], core_ids=[0])
    return result.results[0]["out"]
```

```python
from contextlib import ExitStack

import concourse.bass as bass
from concourse import mybir

P = 128
G = 8
SUPER = P * G
WINDOW = 48
C = 8
F = 32
H = 16
L1, L2 = 512, 384
PIECES = 6
KH = PIECES * H
EPS = 1e-5

ALU = mybir.AluOpType
ACT = mybir.ActivationFunctionType
AX = mybir.AxisListType
F32 = mybir.dt.float32
BF16 = mybir.dt.bfloat16
I32 = mybir.dt.int32
RMAX = bass.bass_isa.ReduceOp.max


def build_gnn_layer(nc, x, src, dst, emb_t, vec, weight, fc1_w1, fc1_w2, fc2_w1, fc2_w2, out):
    N = x.shape[0]
    E = src.shape[0]
    K1 = emb_t.shape[0]
    FULL = E // SUPER
    NS = FULL + (1 if E % SUPER else 0)
    REPEATED = NS * SUPER - E
    NB = -(-N // P)
    NW = -(-N // WINDOW)
    ACC = max(NB * P, NW * WINDOW) + WINDOW
    SCAN = -(-FULL // P)
    assert FULL >= 8 and NS <= 512 and SCAN * SUPER + SUPER <= ACC

    c1 = 1.0 / (4.0 * 32.0 ** 0.5)
    c2 = 1.0 / (4.0 * 4.0)
    r3 = 3.0 ** 0.5

    def rows(ap, width):
        flat = ap[0:FULL * SUPER] if width == 1 else ap[0:FULL * SUPER, :]
        pat = "(s p t) -> s p t" if width == 1 else "(s p t) k -> s p (t k)"
        return flat.rearrange(pat, p=P, t=G)

    def last_rows(ap, width):
        flat = ap[E - SUPER:E] if width == 1 else ap[E - SUPER:E, :]
        pat = "(p t) -> p t" if width == 1 else "(p t) k -> p (t k)"
        return flat.rearrange(pat, t=G)

    src_rows, dst_rows, wgt_rows, vec_rows = rows(src, 1), rows(dst, 1), rows(weight, 1), rows(vec, 3)
    emb_cols = emb_t[:, 0:FULL * SUPER].rearrange("k (s e) -> s k e", e=SUPER)

    with ExitStack() as ctx:
        def sb(name, shape, dt=F32):
            return ctx.enter_context(nc.sbuf_tensor(name, shape, dt))

        def sem(name):
            return ctx.enter_context(nc.semaphore(name))

        identity = sb("identity", [P, P])
        identity_bf = sb("identity_bf", [P, P], BF16)
        node_iota_i = sb("node_iota_i", [P, WINDOW], I32)
        node_iota = sb("node_iota", [P, WINDOW])
        edge_iota_i = sb("edge_iota_i", [P, G], I32)
        fresh = sb("fresh", [P, G])
        ones_row = sb("ones_row", [1, P])
        w1 = sb("w1", [K1, 2 * H])
        w2 = sb("w2", [H, L1 + L2])
        w2_parts = sb("w2_parts", [H, 3, L1 + L2], BF16)
        w2_stack = sb("w2_stack", [KH, L1 + L2], BF16)
        base_i = sb("base_i", [1, NS], I32)
        base_row = sb("base_row", [1, NS])
        base = sb("base", [P, NS])
        span = sb("span", [P, 3, SCAN + 1])
        excess = sb("excess", [P, SCAN + 1])
        excess_low = sb("excess_low", [P, SCAN + 1])
        excess_one = sb("excess_one", [P, 1])
        excess_all = sb("excess_all", [P, 1])
        general = sb("general", [P, 1], I32)

        idx = sb("idx", [P, 2, 2, G], I32)
        emb = sb("emb", [K1, 2, SUPER])
        vecs = sb("vecs", [P, 2, G, 3])
        late = sb("late", [P, 2, G])
        late_dst = sb("late_dst", [P, 2, G], I32)
        nodes = sb("nodes", [P, 2, G, 2, F])
        inv = sb("inv", [P, NS * G])
        r = sb("r", [P, 2, G, 3])
        S = sb("S", [P, 2, G, 4 * C])
        V = sb("V", [P, 2, G, 3, 2 * C])
        vr = sb("vr", [P, G, 3, 2 * C])
        hid = sb("hid", [P, 2 * G, H])
        hid_rest = sb("hid_rest", [P, 2 * G, H])
        hid_parts = sb("hid_parts", [P, 2, 2 * G, KH], BF16)
        hid_t = sb("hid_t", [KH, 3, G, P], BF16)
        wa = sb("wa", [P, 2, G, L1])
        wb = sb("wb", [P, G, L2])
        prod_v = sb("prod_v", [P, G, 3, 2 * C, C])
        sv = sb("sv", [P, G, C])
        M = sb("M", [P, G, 2 * C])
        VT = sb("VT", [P, G, 3, C])
        vtr = sb("vtr", [P, G, 3, C])
        prod_g = sb("prod_g", [P, G, 2, 2 * C, C])
        prod_o = sb("prod_o", [P, G, 4, C, C])
        osum = sb("osum", [P, G, 4, C])
        th = sb("th", [P, G, 2, C])
        q = sb("q", [P, G, 3, C])
        msg = sb("msg", [P, G, F + C])
        rel = sb("rel", [P, 2, G])
        rel_raw = sb("rel_raw", [P, G])
        hot = sb("hot", [P, 2, G, WINDOW])
        acc = sb("acc", [P, ACC])

        xn = sb("xn", [P, NB, F])
        mean = sb("mean", [P, NB])
        var = sb("var", [P, NB])

        pw = ctx.enter_context(nc.psum_tensor("pw", [P, 2, 2, 512], F32))
        pt = ctx.enter_context(nc.psum_tensor("pt", [KH, G, P], BF16))
        ph = ctx.enter_context(nc.psum_tensor("ph", [P, 512], F32))
        p1 = ctx.enter_context(nc.psum_tensor("p1", [P, 512], F32))
        p2 = ctx.enter_context(nc.psum_tensor("p2", [P, 512], F32))
        hid_ps = ph[:, 0:G * 2 * H].rearrange("p (t h) -> p t h", h=2 * H)
        vs_ps = p1[:, 0:G * 3 * C].rearrange("p (t k w) -> p t k w", k=3, w=C)
        st_ps = p1[:, G * 3 * C:G * 5 * C].rearrange("p (t a w) -> p t a w", a=2, w=C)
        gates_ps = p2[:, 0:G * 2 * C].rearrange("p (t a w) -> p t a w", a=2, w=C)
        scat_ps = ph[0:F, G * 2 * H:G * 2 * H + WINDOW]

        s_const = sem("s_const")
        s_w_in = sem("s_w_in")
        s_base_in = sem("s_base_in")
        s_scan_in = sem("s_scan_in")
        s_pre = sem("s_pre")
        s_parts = sem("s_parts")
        s_stack = sem("s_stack")
        s_base_row = sem("s_base_row")
        s_base_ps = sem("s_base_ps")
        s_excess = sem("s_excess")
        s_excess_all = sem("s_excess_all")
        s_general = sem("s_general")
        idx_in = [sem(f"idx_in{i}") for i in range(2)]
        emb_in = [sem(f"emb_in{i}") for i in range(2)]
        vec_in = [sem(f"vec_in{i}") for i in range(2)]
        wgt_in = [sem(f"wgt_in{i}") for i in range(2)]
        late_in = [sem(f"late_in{i}") for i in range(2)]
        nodes_in = [[sem(f"nodes_in{i}{k}") for k in range(2)] for i in range(2)]
        s_all_vec = sem("s_all_vec")
        s_norm2 = sem("s_norm2")
        s_length = sem("s_length")
        s_inv = sem("s_inv")
        r_done = sem("r_done")
        sv_copied = sem("sv_copied")
        vr_done = sem("vr_done")
        vdot_done = sem("vdot_done")
        hid_mm = sem("hid_mm")
        hid_done = sem("hid_done")
        hid_a = sem("hid_a")
        hid_b = sem("hid_b")
        hid_rest_done = sem("hid_rest_done")
        hid_c = sem("hid_c")
        turned = sem("turned")
        turned_out = sem("turned_out")
        wa_mm = sem("wa_mm")
        wa_out = sem("wa_out")
        wb_mm = sem("wb_mm")
        wb_out = sem("wb_out")
        pv_done = sem("pv_done")
        ps_done = sem("ps_done")
        p2_done = sem("p2_done")
        sv_done = sem("sv_done")
        vs_sum = sem("vs_sum")
        st_sum = sem("st_sum")
        m_st = sem("m_st")
        vt_part = sem("vt_part")
        vt_done = sem("vt_done")
        vtr_done = sem("vtr_done")
        m_vd = sem("m_vd")
        pg_done = sem("pg_done")
        po_done = sem("po_done")
        osum_done = sem("osum_done")
        gates_sum = sem("gates_sum")
        tanh_done = sem("tanh_done")
        q_done = sem("q_done")
        msg_done = sem("msg_done")
        rel_raw_done = sem("rel_raw_done")
        rel_done = sem("rel_done")
        hot_done = sem("hot_done")
        scat_mm = sem("scat_mm")
        acc_done = sem("acc_done")
        rel_kept = sem("rel_kept")
        rel_moved = sem("rel_moved")
        gathers_begun = sem("gathers_begun")
        windows_begun_pe = sem("windows_begun_pe")
        windows_begun_dve = sem("windows_begun_dve")
        xn_in = sem("xn_in")
        turn_acc = sem("turn_acc")
        post = sem("post")
        root_done = sem("root_done")
        out_done = sem("out_done")

        class At:

            def __init__(self, b, d):
                self.b, self.par, self.half = b, d % 2, b + d // 2
                self.static = isinstance(b, int)
                self.d = d

            def n(self, per=1, more=0):
                return self.b * (2 * per) + (self.d * per + more)

            def k(self, per, more=0):
                return self.b * per + (per * (self.d // 2 + 1) + more)

            def before(self, by):
                return At(self.b, self.d - by)

            def index(self):
                return self.b * 2 + self.d

            def is_last(self):
                return self.static and 2 * self.b + self.d == NS - 1 and NS != FULL

        def wait(eng, semaphore, value):
            if isinstance(value, int) and value <= 0:
                return
            eng.wait_ge(semaphore, value)

        def periods(eng, body):
            first = 4
            pairs = (FULL - 3 - first) // 2
            for i in range(-2, first):
                body(At(0, i), i)
            with eng.Fori(0, pairs) as b:
                body(At(b + first // 2, 0), None)
                body(At(b + first // 2, 1), None)
            for i in range(first + 2 * pairs, NS + 2):
                body(At(i // 2, i % 2), i)

        def stage(at, by, i):
            if i is not None and not 0 <= i + by < NS:
                return None
            return At(at.b, at.d + by)

        wa_flat = wa[:, :, :, :].rearrange("p b t w -> p (b t w)")
        in_wa = min(FULL, 2 * G * L1 // (3 * G))
        room = [(wa_flat, 0, in_wa)]
        if FULL > in_wa:
            room.append((prod_v[:, :, :, :, :].rearrange("p a b c d -> p (a b c d)"), in_wa, FULL))
        all_vectors = room
        last_vectors = prod_g[:, :, :, :, :].rearrange("p a b c d -> p (a b c d)")[:, 0:3 * G]
        assert (FULL - in_wa) * 3 <= 3 * 2 * C * C

        block = ctx.enter_context(nc.Block())

        @block.sync
        def _(sp):
            def load_early(a):
                p, s, two, last = a.par, a.index(), a.before(2), a.is_last()
                for k in range(2):
                    wait(sp, nodes_in[p][k], two.k(16 * G))
                sp.dma_start(idx[:, p, 0, :], last_rows(src, 1) if last else src_rows[s]).then_inc(idx_in[p], 16)
                sp.dma_start(idx[:, p, 1, :], last_rows(dst, 1) if last else dst_rows[s]).then_inc(idx_in[p], 16)
                wait(sp, hid_mm, two.n(1, 1))
                sp.dma_start(emb[:, p, :], emb_t[:, E - SUPER:E] if last else emb_cols[s]).then_inc(emb_in[p], 16)

            load_early(At(0, 0))
            sp.dma_start(w1[:, 0:H], fc1_w1).then_inc(s_w_in, 16)
            sp.dma_start(w1[:, H:2 * H], fc2_w1).then_inc(s_w_in, 16)
            sp.dma_start(w2[:, 0:L1], fc1_w2).then_inc(s_w_in, 16)
            sp.dma_start(w2[:, L1:L1 + L2], fc2_w2).then_inc(s_w_in, 16)
            sp.dma_start(base_i[0:1, 0:FULL], dst[0:FULL * SUPER].rearrange("(a s e) -> a s e", a=1, e=SUPER)[:, :, 0],
                         allow_slow_non_contiguous=True).then_inc(s_base_in, 16)
            if NS != FULL:
                sp.dma_start(base_i[0:1, FULL:NS], dst[E - SUPER:E - SUPER + 1].rearrange("(a s) -> a s", a=1)
                             ).then_inc(s_base_in, 16)
            scan = acc[:, :].bitcast(I32)
            for c in range(SCAN):
                n = min(P, FULL - c * P)
                sp.dma_start(scan[0:n, c * SUPER:(c + 1) * SUPER],
                             dst[c * P * SUPER:(c * P + n) * SUPER].rearrange("(s e) -> s e", e=SUPER)
                             ).then_inc(s_scan_in, 16)
            sp.dma_start(scan[0:1, SCAN * SUPER:(SCAN + 1) * SUPER],
                         dst[E - SUPER:E].rearrange("(a e) -> a e", a=1)).then_inc(s_scan_in, 16)

            for buf, lo, hi in all_vectors:
                sp.dma_start(buf[:, 0:3 * G * (hi - lo)].rearrange("p (s c) -> p s c", c=3 * G),
                             vec_rows[lo:hi].rearrange("s p c -> p s c")).then_inc(s_all_vec, 16)
            if NS != FULL:
                sp.dma_start(last_vectors, last_rows(vec, 3)).then_inc(s_all_vec, 16)

            def load_vectors(a):
                p, s, two, last = a.par, a.index(), a.before(2), a.is_last()
                wait(sp, r_done, two.n(1, 1))
                sp.dma_start(vecs[:, p, :, :].rearrange("p t k -> p (t k)"),
                             last_rows(vec, 3) if last else vec_rows[s]).then_inc(vec_in[p], 16)

            def load_weights(a):
                p, s, two, last = a.par, a.index(), a.before(2), a.is_last()
                wait(sp, msg_done, two.n(2, 2))
                sp.dma_start(late[:, p, :], last_rows(weight, 1) if last else wgt_rows[s]).then_inc(wgt_in[p], 16)

            def load_destinations(a):
                p, s, two, last = a.par, a.index(), a.before(2), a.is_last()
                wait(sp, rel_done, two.n(1, 1))
                sp.dma_start(late_dst[:, p, :], last_rows(dst, 1) if last else dst_rows[s]).then_inc(late_in[p], 16)

            sp.wait_ge(s_parts, 1)
            for g, part in enumerate((0, 1, 2, 0, 1, 0)):
                sp.dma_start(w2_stack[H * g:H * g + H, :], w2_parts[:, part, :]).then_inc(s_stack, 16)

            def body(at, i):
                for load, ahead in ((load_early, 3), (load_vectors, 2), (load_destinations, 1), (load_weights, 0)):
                    a = stage(at, ahead, i)
                    if a is not None:
                        load(a)

            periods(sp, body)
            whole = N // NB
            sp.dma_start(xn[0:whole, :, :].rearrange("p b f -> p (b f)"),
                         x[0:whole * NB, :].rearrange("(p b) f -> p (b f)", b=NB)).then_inc(xn_in, 16)
            if N > whole * NB:
                sp.dma_start(xn[whole:whole + 1, 0:N - whole * NB, :].rearrange("p b f -> p (b f)"),
                             x[whole * NB:N, :].rearrange("(p b) f -> p (b f)", p=1)).then_inc(xn_in, 16)
            sp.wait_ge(post, 9)
            sp.dma_start(out[0:whole * NB, :].rearrange("(p b) f -> p (b f)", b=NB),
                         xn[0:whole, :, :].rearrange("p b f -> p (b f)")).then_inc(out_done, 16)
            if N > whole * NB:
                sp.dma_start(out[whole * NB:N, :].rearrange("(p b) f -> p (b f)", p=1),
                             xn[whole:whole + 1, 0:N - whole * NB, :].rearrange("p b f -> p (b f)")
                             ).then_inc(out_done, 16)
            sp.wait_ge(out_done, 32 if N > whole * NB else 16)

        @block.gpsimd
        def _(pool):
            nc.gpsimd.memset(identity[:, :], 0.0).then_inc(s_const, 1)
            nc.gpsimd.memset(identity_bf[:, :], 0.0).then_inc(s_const, 1)
            nc.gpsimd.memset(ones_row[:, :], 1.0).then_inc(s_const, 1)
            nc.gpsimd.iota(node_iota_i[:, :], pattern=[[1, WINDOW]], base=0, channel_multiplier=0).then_inc(s_const, 1)
            nc.gpsimd.iota(edge_iota_i[:, :], pattern=[[1, G]], base=0, channel_multiplier=G).then_inc(s_const, 1)
            nc.gpsimd.memset(xn[:, :, :], 0.0).then_inc(s_const, 1)
            pool.wait_ge(s_const, 6)
            for m in (identity, identity_bf):
                nc.gpsimd.affine_select(out=m[:, :], in_=m[:, :], compare_op=ALU.not_equal, fill=1.0, base=0,
                                        pattern=[[-1, P]], channel_multiplier=1).then_inc(s_const, 1)

            def split(a):
                pool.wait_ge(hid_a, a.n(1, 1))
                wait(pool, hid_b, a.n())
                nc.gpsimd.tensor_tensor(hid_rest[:, :, :], hid[:, :, :], hid_parts[:, a.par, :, 0:H],
                                        ALU.subtract).then_inc(hid_rest_done, 1)

            def gathers(a):
                p = a.par
                pool.wait_ge(idx_in[p], a.k(32))
                wait(pool, sv_copied, a.before(2).n(4, 4))
                pool.sem_inc(gathers_begun, 1)
                for side in range(2):
                    for t in range(G):
                        nc.gpsimd.indirect_dma_start(
                            nodes[:, p, t, side, :], None, x,
                            bass.IndirectOffsetOnAxis(ap=idx[:, p, side, t:t + 1], axis=0)
                        ).then_inc(nodes_in[p][side], 16)
                    if side == 0:
                        split(a)

            def along(a):
                p = a.par
                pool.wait_ge(r_done, a.n(1, 1))
                pool.wait_ge(sv_copied, a.n(4, 4))
                wait(pool, vdot_done, a.n())
                nc.gpsimd.tensor_tensor(vr[:, :, :, :], V[:, p, :, :, :],
                                        r[:, p, :, :].unsqueeze(3).broadcast_to([P, G, 3, 2 * C]),
                                        ALU.mult).then_inc(vr_done, 1)

            pool.wait_ge(s_excess, 1)
            nc.gpsimd.partition_all_reduce(excess_all[:, :], excess_one[:, :], P, RMAX).then_inc(s_excess_all, 1)

            def body(at, i):
                a = stage(at, 0, i)
                if a is not None:
                    along(a)
                a = stage(at, 2, i)
                if a is not None:
                    gathers(a)

            periods(pool, body)

        @block.scalar
        def _(act):
            def rows_laid_out(a):
                p = a.par
                wait(act, ps_done, a.before(2).n(1, 1))
                for side in range(2):
                    act.wait_ge(nodes_in[p][side], a.k(16 * G))
                    c = slice(C * side, C * side + C)
                    nc.scalar.activation(S[:, p, :, c], nodes[:, p, :, side, 0:C], ACT.Copy).then_inc(sv_copied, 1)
                    nc.scalar.activation(V[:, p, :, :, c],
                                         nodes[:, p, :, side, C:F].rearrange("p t (u k) -> p t k u", k=3),
                                         ACT.Copy).then_inc(sv_copied, 1)

            def hidden_parts(a):
                act.wait_ge(hid_mm, a.n(1, 1))
                wait(act, hid_rest_done, a.n())
                nc.scalar.activation(hid[:, :, :].rearrange("p (t l) h -> p t (l h)", l=2), hid_ps, ACT.Relu,
                                     scale=float(K1) ** -0.5).then_inc(hid_done, 1)
                act.wait_ge(hid_done, a.n(1, 1))
                wait(act, turned, a.n(2, -2))
                parts = hid_parts[:, a.par, :, :].rearrange("p a (g h) -> p a g h", h=H)
                nc.scalar.activation(parts[:, :, 0:3, :], hid[:, :, :].unsqueeze(2).broadcast_to([P, 2 * G, 3, H]),
                                     ACT.Copy).then_inc(hid_a, 1)

            def hidden_second(a):
                parts = hid_parts[:, a.par, :, :].rearrange("p a (g h) -> p a g h", h=H)
                act.wait_ge(hid_rest_done, a.n(1, 1))
                nc.scalar.activation(parts[:, :, 3:5, :], hid_rest[:, :, :].unsqueeze(2).broadcast_to([P, 2 * G, 2, H]),
                                     ACT.Copy).then_inc(hid_b, 1)

            def turned_copy(a, layer):
                act.wait_ge(turned, a.n(2, layer + 1))
                wait(act, (wa_mm, wb_mm)[layer], a.n(4, -4 * layer))
                nc.scalar.activation(hid_t[:, layer and 1 + a.par, :, :], pt[:, :, :], ACT.Copy).then_inc(turned_out, 1)

            def weights_out(a, layer, pairs):
                buf, width, made, taken = ((wa[:, a.par], L1, wa_mm, wa_out), (wb[:, :, :], L2, wb_mm, wb_out))[layer]
                if layer == 0:
                    wait(act, st_sum, a.n(1, -1))
                    wait(act, sv_done, a.n(1, -1))
                else:
                    wait(act, osum_done, a.n())
                for pair in pairs:
                    act.wait_ge(made, a.n(4, pair + 1))
                    nc.scalar.activation(buf[:, 2 * pair:2 * pair + 2, :], pw[:, pair % 2, :, 0:width],
                                         ACT.Copy).then_inc(taken, 1)

            def tanhs(a):
                act.wait_ge(gates_sum, a.n(1, 1))
                wait(act, msg_done, a.n(2))
                nc.scalar.activation(th[:, :, :, :], gates_ps, ACT.Tanh).then_inc(tanh_done, 1)

            def body(at, i):
                zero, one, three = stage(at, 2, i), stage(at, 1, i), stage(at, -1, i)
                if i == -1:
                    act.wait_ge(s_norm2, 1)
                    nc.scalar.activation(inv[:, :], inv[:, :], ACT.Sqrt).then_inc(s_length, 1)
                if three is not None:
                    weights_out(three, 1, (0, 1))
                if one is not None:
                    turned_copy(one, 0)
                if three is not None:
                    weights_out(three, 1, (2, 3))
                if zero is not None:
                    hidden_parts(zero)
                if one is not None:
                    rows_laid_out(one)
                if zero is not None:
                    hidden_second(zero)
                if one is not None:
                    turned_copy(one, 1)
                if one is not None:
                    weights_out(one, 0, (0, 1, 2, 3))
                if three is not None:
                    tanhs(three)

            periods(act, body)
            act.wait_ge(post, 6)
            nc.scalar.activation(var[:, :], var[:, :], ACT.Sqrt).then_inc(root_done, 1)

        @block.tensor
        def _(pe):
            pe.wait_ge(s_const, 8)
            pe.wait_ge(s_base_row, 1)
            nc.tensor.matmul(ph[:, 0:NS], ones_row[:, :], base_row[:, :], start=True, stop=True).then_inc(s_base_ps, 1)
            pe.wait_ge(s_general, 1)
            pe.wait_ge(s_w_in, 64)
            pe.wait_ge(s_stack, 16 * PIECES)
            flag = nc.tensor.value_load(general[0:1, 0:1], min_val=0, max_val=1)

            def hidden(a, windows, more):
                p = a.par
                pe.wait_ge(emb_in[p], a.k(16))
                wait(pe, hid_done, a.n())
                wait(pe, acc_done, a.n(windows, more - 4 * windows))
                for t in range(G):
                    mm = nc.tensor.matmul(hid_ps[:, t, :], emb[:, p, t:SUPER:G], w1[:, :], start=True, stop=True)
                mm.then_inc(hid_mm, 1)

            def turn(a, layer):
                pe.wait_ge(hid_a, a.n(1, 1))
                pe.wait_ge(hid_b, a.n(1, 1))
                pe.wait_ge(hid_c, a.n(1, 1))
                wait(pe, turned_out, a.n(2, layer))
                for t in range(G):
                    mm = nc.tensor.transpose(pt[:, t, :], hid_parts[:, a.par, 2 * t + layer, :], identity_bf[:, :])
                mm.then_inc(turned, 1)

            def edge_weights(a, layer, pairs, free):
                made, taken = ((wa_mm, wa_out), (wb_mm, wb_out))[layer]
                lo, width = ((0, L1), (L1, L2))[layer]
                pe.wait_ge(turned_out, a.n(2, layer + 1))
                for pair in pairs:
                    if pair == 0:
                        wait(pe, *free)
                    if pair >= 2:
                        pe.wait_ge(taken, a.n(4, pair - 1))
                    for t in range(2):
                        mm = nc.tensor.matmul(pw[:, pair % 2, t, 0:width], hid_t[:, layer and 1 + a.par, 2 * pair + t, :],
                                              w2_stack[:, lo:lo + width], start=True, stop=True)
                    mm.then_inc(made, 1)

            def vector_sums(a):
                pe.wait_ge(pv_done, a.n(1, 1))
                wait(pe, vt_done, a.n())
                wait(pe, m_st, a.n())
                for u in range(2 * C):
                    mm = nc.tensor.matmul(vs_ps, identity[:, :], prod_v[:, :, :, u, :],
                                          start=(u == 0), stop=(u == 2 * C - 1))
                mm.then_inc(vs_sum, 1)

            def scalar_sums(a):
                pe.wait_ge(ps_done, a.n(1, 1))
                prods = wa[:, a.par, :, 0:256].rearrange("p t (a u w) -> p t a u w", a=2, w=C)
                for u in range(2 * C):
                    mm = nc.tensor.matmul(st_ps, identity[:, :], prods[:, :, :, u, :],
                                          start=(u == 0), stop=(u == 2 * C - 1))
                mm.then_inc(st_sum, 1)

            def gate_sums(a):
                pe.wait_ge(pg_done, a.n(1, 1))
                wait(pe, tanh_done, a.n())
                for u in range(2 * C):
                    mm = nc.tensor.matmul(gates_ps, identity[:, :], prod_g[:, :, :, u, :],
                                          start=(u == 0), stop=(u == 2 * C - 1))
                mm.then_inc(gates_sum, 1)

            def window(par):
                for t in range(G):
                    mm = nc.tensor.matmul(scat_ps, msg[:, t, 0:F], hot[:, par, t, :], start=(t == 0), stop=(t == G - 1))
                mm.then_inc(scat_mm, 1)

            def scatter(a, is_general):
                pe.wait_ge(msg_done, a.n(2, 2))
                ahead = a.n(1, 5)
                pe.wait_ge(hid_done, min(ahead, NS) if a.static else ahead)
                if not is_general:
                    pe.wait_ge(hot_done, a.n(1, 1))
                    wait(pe, acc_done, a.n())
                    window(a.par)
                    return
                pe.sem_inc(windows_begun_pe, 1)
                with pe.Fori(0, NW) as w:
                    pe.wait_ge(hot_done, a.n(NW, 1) + w)
                    pe.wait_ge(acc_done, a.n(NW, 1) + w)
                    window(a.par)

            def program(is_general):
                def body(at, i):
                    zero, one, two, three, four = (stage(at, by, i) for by in (2, 1, 0, -1, -2))
                    if three is not None:
                        for_wb = (wa_out, three.n(4, 8) if two is not None else three.n(4, 4))
                        edge_weights(three, 1, (0, 1), for_wb)
                    if one is not None:
                        turn(one, 0)
                    if zero is not None:
                        hidden(zero, NW if is_general else 1, int(is_general))
                    if three is not None:
                        edge_weights(three, 1, (2, 3), for_wb)
                    if two is not None:
                        vector_sums(two)
                    if one is not None:
                        turn(one, 1)
                    if one is not None:
                        for_wa = (wb_out, one.n(4, -4))
                        edge_weights(one, 0, (0, 1), for_wa)
                    if two is not None:
                        scalar_sums(two)
                    if one is not None:
                        edge_weights(one, 0, (2, 3), for_wa)
                    if four is not None:
                        scatter(four, is_general)
                    if three is not None:
                        gate_sums(three)
                periods(pe, body)

            with pe.If(flag == 0):
                program(False)
            with pe.If(flag != 0):
                pe.sem_inc(scat_mm, 1)
                program(True)
            pe.wait_ge(post, 1)
            banks = (pw[:, 0, 0, :], pw[:, 0, 1, :], pw[:, 1, 0, :], pw[:, 1, 1, :], ph[:, :], p1[:, :], p2[:, :])
            per = 512 // F
            for b in range(NB):
                mm = nc.tensor.transpose(banks[b // per][:, F * (b % per):F * (b % per) + F],
                                         acc[0:F, b:b + NB * (P - 1) + 1:NB], identity[0:F, 0:F])
            mm.then_inc(turn_acc, 1)

        @block.vector
        def _(dve):
            steps = [0]

            def done(ins):
                steps[0] += 1
                ins.then_inc(s_pre, 1)
                dve.wait_ge(s_pre, steps[0])

            dve.wait_ge(s_w_in, 64)
            w2_rest = prod_o[0:H, :, :, :, :].rearrange("p a b c d -> p (a b c d)")[:, 0:L1 + L2]
            done(nc.vector.tensor_scalar(w2[:, 0:256], w2[:, 0:256], c1, None, ALU.mult))
            done(nc.vector.tensor_scalar(w2[:, 256:384], w2[:, 256:384], c1 * r3, None, ALU.mult))
            done(nc.vector.tensor_scalar(w2[:, 384:L1], w2[:, 384:L1], c1, None, ALU.mult))
            done(nc.vector.tensor_scalar(w2[:, L1:L1 + 256], w2[:, L1:L1 + 256], c2, None, ALU.mult))
            done(nc.vector.tensor_scalar(w2[:, L1 + 256:L1 + 320], w2[:, L1 + 256:L1 + 320], c2 * r3, None, ALU.mult))
            done(nc.vector.tensor_scalar(w2[:, L1 + 320:L1 + L2], w2[:, L1 + 320:L1 + L2], c2, None, ALU.mult))
            done(nc.vector.tensor_copy(w2_parts[:, 0, :], w2[:, :]))
            done(nc.vector.tensor_tensor(w2_rest, w2[:, :], w2_parts[:, 0, :], ALU.subtract))
            done(nc.vector.tensor_copy(w2_parts[:, 1, :], w2_rest))
            nc.vector.tensor_tensor(w2_parts[:, 2, :], w2_rest, w2_parts[:, 1, :],
                                    ALU.subtract).then_inc(s_parts, 1)
            dve.wait_ge(s_base_in, 32 if NS != FULL else 16)
            nc.vector.tensor_copy(base_row[:, :], base_i[:, :]).then_inc(s_base_row, 1)
            done(nc.vector.memset(span[:, :, :], 0.0))
            dve.wait_ge(s_scan_in, 16 * (SCAN + 1))
            scan = acc[:, :].bitcast(I32)
            for c in range(SCAN + 1):
                n = min(P, FULL - c * P) if c < SCAN else 1
                part = scan[0:n, c * SUPER:(c + 1) * SUPER]
                done(nc.vector.tensor_reduce(span[0:n, 0, c:c + 1], part, AX.X, ALU.max))
                done(nc.vector.tensor_reduce(span[0:n, 1, c:c + 1], part, AX.X, ALU.min))
                done(nc.vector.tensor_copy(span[0:n, 2, c:c + 1], part[:, 0:1]))
            done(nc.vector.tensor_tensor(excess[:, :], span[:, 0, :], span[:, 2, :], ALU.subtract))
            done(nc.vector.tensor_scalar(excess[:, :], excess[:, :], -(WINDOW - 1.0), None, ALU.add))
            done(nc.vector.tensor_tensor(excess_low[:, :], span[:, 2, :], span[:, 1, :], ALU.subtract))
            done(nc.vector.tensor_tensor(excess[:, :], excess[:, :], excess_low[:, :], ALU.max))
            nc.vector.tensor_reduce(excess_one[:, :], excess[:, :], AX.X, ALU.max).then_inc(s_excess, 1)
            done(nc.vector.memset(acc[:, :], 0.0))
            dve.wait_ge(s_const, 8)
            done(nc.vector.tensor_copy(node_iota[:, :], node_iota_i[:, :]))
            done(nc.vector.tensor_scalar(fresh[:, :], edge_iota_i[:, :], float(REPEATED), None, ALU.is_ge))
            dve.wait_ge(s_base_ps, 1)
            done(nc.vector.tensor_copy(base[:, :], ph[:, 0:NS]))
            dve.wait_ge(s_excess_all, 1)
            nc.vector.tensor_scalar(general[:, :], excess_all[:, :], 0.0, None, ALU.is_gt).then_inc(s_general, 1)
            dve.wait_ge(s_general, 1)
            flag = nc.vector.value_load(general[0:1, 0:1], min_val=0, max_val=1)

            dve.wait_ge(s_all_vec, 16 * (len(all_vectors) + (NS != FULL)))
            for buf, lo, hi in all_vectors + ([(last_vectors, FULL, NS)] if NS != FULL else []):
                part = buf[:, 0:3 * G * (hi - lo)]
                done(nc.vector.tensor_tensor(part, part, part, ALU.mult))
                done(nc.vector.tensor_reduce(inv[:, G * lo:G * hi], part.rearrange("p (e k) -> p e k", k=3), AX.X, ALU.add))
            nc.vector.memset(osum[:, :, :, :], 0.0).then_inc(s_norm2, 1)

            def inverse(c0, c1):
                nc.vector.reciprocal(inv[:, c0:c1], inv[:, c0:c1]).then_inc(s_inv, 1)

            def split_again(a):
                dve.wait_ge(hid_b, a.n(1, 1))
                nc.vector.tensor_tensor(hid_parts[:, a.par, :, KH - H:KH], hid_rest[:, :, :],
                                        hid_parts[:, a.par, :, 3 * H:4 * H], ALU.subtract).then_inc(hid_c, 1)

            def vdots(a):
                dve.wait_ge(vr_done, a.n(1, 1))
                nc.vector.tensor_reduce(S[:, a.par, :, 2 * C:4 * C], vr[:, :, :, :].rearrange("p t k u -> p t u k"),
                                        AX.X, ALU.add).then_inc(vdot_done, 1)

            def directions(a):
                p = a.par
                dve.wait_ge(vec_in[p], a.k(16))
                wait(dve, q_done, a.n(2, -3))
                wait(dve, vr_done, a.n(1, -1))
                here = bass.ds(a.index() * G, G) if not a.static else slice(a.index() * G, a.index() * G + G)
                nc.vector.tensor_tensor(r[:, p, :, :], vecs[:, p, :, :],
                                        inv[:, here].unsqueeze(2).broadcast_to([P, G, 3]), ALU.mult).then_inc(r_done, 1)

            def vector_products(a):
                p = a.par
                dve.wait_ge(wa_out, a.n(4, 4))
                dve.wait_ge(sv_copied, a.n(4, 4))
                wait(dve, vs_sum, a.n())
                nc.vector.tensor_tensor(
                    prod_v[:, :, :, :, :],
                    wa[:, p, :, 384:L1].rearrange("p t (u w) -> p t u w", w=C).unsqueeze(2).broadcast_to([P, G, 3, 2 * C, C]),
                    V[:, p, :, :, :].unsqueeze(4).broadcast_to([P, G, 3, 2 * C, C]), ALU.mult).then_inc(pv_done, 1)

            def scalar_products(a):
                p = a.par
                third = wa[:, p, :, 256:384].rearrange("p t (u w) -> p t u w", w=C)
                nc.vector.tensor_tensor(
                    third, third, S[:, p, :, 0:2 * C].unsqueeze(3).broadcast_to([P, G, 2 * C, C]),
                    ALU.mult).then_inc(p2_done, 1)
                dve.wait_ge(vdot_done, a.n(1, 1))
                both = wa[:, p, :, 0:256].rearrange("p t (u w) -> p t u w", w=C)
                nc.vector.tensor_tensor(
                    both, both,
                    S[:, p, :, :].unsqueeze(3).broadcast_to([P, G, 4 * C, C]), ALU.mult).then_inc(ps_done, 1)

            def third_sum(a):
                dve.wait_ge(p2_done, a.n(1, 1))
                nc.vector.tensor_reduce(sv[:, :, :], wa[:, a.par, :, 256:384].rearrange("p t (u w) -> p t w u", w=C),
                                        AX.X, ALU.add).then_inc(sv_done, 1)

            def destinations(a, is_general):
                p = a.par
                dve.wait_ge(late_in[p], a.k(16))
                if is_general:
                    wait(dve, rel_moved, a.n(NW, 1 - NW))
                first = 0.0 if is_general else base[:, bass.ds(a.index(), 1)] if not a.static else base[:, a.index():a.index() + 1]
                if not a.is_last():
                    nc.vector.tensor_scalar(rel[:, p, :], late_dst[:, p, :], first, None, ALU.subtract).then_inc(rel_done, 1)
                    return
                nc.vector.tensor_scalar(rel_raw[:, :], late_dst[:, p, :], first, None, ALU.subtract).then_inc(rel_raw_done, 1)
                dve.wait_ge(rel_raw_done, 1)
                nc.vector.scalar_tensor_tensor(rel[:, p, :], rel_raw[:, :], 1.0, fresh[:, :], ALU.add,
                                               ALU.mult).then_inc(rel_kept, 1)
                dve.wait_ge(rel_kept, 1)
                nc.vector.tensor_scalar(rel[:, p, :], rel[:, p, :], -1.0, None, ALU.add).then_inc(rel_done, 1)

            def one_hot(par):
                return nc.vector.tensor_tensor(
                    hot[:, par, :, :], node_iota[:, :].unsqueeze(1).broadcast_to([P, G, WINDOW]),
                    rel[:, par, :].unsqueeze(2).broadcast_to([P, G, WINDOW]), ALU.is_equal)

            def products2(a):
                dve.wait_ge(wb_out, a.n(4, 4))
                dve.wait_ge(m_st, a.n(1, 1))
                dve.wait_ge(m_vd, a.n(1, 1))
                wait(dve, gates_sum, a.n())
                for half in range(2):
                    ins = nc.vector.tensor_tensor(
                        prod_g[:, :, half, :, :],
                        wb[:, :, 128 * half:128 * half + 128].rearrange("p t (u w) -> p t u w", w=C),
                        M[:, :, :].unsqueeze(3).broadcast_to([P, G, 2 * C, C]), ALU.mult)
                ins.then_inc(pg_done, 1)
                nc.vector.tensor_tensor(
                    prod_o[:, :, 0:3, :, :],
                    wb[:, :, 320:L2].rearrange("p t (u w) -> p t u w", w=C).unsqueeze(2).broadcast_to([P, G, 3, C, C]),
                    VT[:, :, :, :].unsqueeze(4).broadcast_to([P, G, 3, C, C]), ALU.mult).then_inc(po_done, 1)
                nc.vector.tensor_tensor(
                    prod_o[:, :, 3, :, :], wb[:, :, 256:320].rearrange("p t (u w) -> p t u w", w=C),
                    M[:, :, 0:C].unsqueeze(3).broadcast_to([P, G, C, C]), ALU.mult).then_inc(po_done, 1)

            def sums2(a):
                dve.wait_ge(po_done, a.n(2, 2))
                nc.vector.tensor_reduce(
                    osum[:, :, :, :].rearrange("p t k w -> p (t k) w"),
                    prod_o[:, :, :, :, :].rearrange("p t k u w -> p (t k) w u"), AX.X, ALU.add).then_inc(osum_done, 1)

            def unit(a):
                return r[:, a.par, :, :].unsqueeze(3).broadcast_to([P, G, 3, C])

            def vt_first(a):
                dve.wait_ge(r_done, a.n(1, 1))
                dve.wait_ge(sv_done, a.n(1, 1))
                wait(dve, po_done, a.n(2))
                nc.vector.tensor_tensor(VT[:, :, :, :], sv[:, :, :].unsqueeze(2).broadcast_to([P, G, 3, C]), unit(a),
                                        ALU.mult).then_inc(vt_part, 1)

            def vt_second(a):
                dve.wait_ge(vs_sum, a.n(1, 1))
                dve.wait_ge(st_sum, a.n(1, 1))
                dve.wait_ge(vt_part, a.n(1, 1))
                nc.vector.tensor_tensor(VT[:, :, :, :], VT[:, :, :, :], vs_ps, ALU.add).then_inc(vt_done, 1)

            def vt_dot_first(a):
                dve.wait_ge(vt_done, a.n(1, 1))
                nc.vector.tensor_tensor(vtr[:, :, :, :], VT[:, :, :, :], unit(a), ALU.mult).then_inc(vtr_done, 1)

            def st_whole(a):
                nc.vector.tensor_reduce(M[:, :, 0:C], st_ps.rearrange("p t a w -> p t w a"), AX.X, ALU.add).then_inc(m_st, 1)

            def vt_dot_second(a):
                dve.wait_ge(vtr_done, a.n(1, 1))
                nc.vector.tensor_reduce(M[:, :, C:2 * C], vtr[:, :, :, :].rearrange("p t k w -> p t w k"), AX.X,
                                        ALU.add).then_inc(m_vd, 1)

            def q_first(a):
                dve.wait_ge(osum_done, a.n(1, 1))
                wait(dve, msg_done, a.n(2))
                nc.vector.tensor_tensor(q[:, :, :, :], osum[:, :, 3, :].unsqueeze(2).broadcast_to([P, G, 3, C]), unit(a),
                                        ALU.mult).then_inc(q_done, 1)

            def q_second(a):
                dve.wait_ge(q_done, a.n(2, 1))
                nc.vector.tensor_tensor(q[:, :, :, :], q[:, :, :, :], osum[:, :, 0:3, :], ALU.add).then_inc(q_done, 1)

            def messages_scalar(a, windows, more):
                p = a.par
                weights = late[:, p, :].unsqueeze(2).unsqueeze(3).broadcast_to([P, G, 2, C])
                dve.wait_ge(wgt_in[p], a.k(16))
                dve.wait_ge(tanh_done, a.n(1, 1))
                wait(dve, scat_mm, a.n(windows, more))
                ends = msg[:, :, :].rearrange("p t (a w) -> p t a w", w=C)[:, :, 0:F // C + 1:F // C, :]
                nc.vector.tensor_tensor(ends, th[:, :, :, :], weights, ALU.mult).then_inc(msg_done, 1)

            def messages_vector(a):
                dve.wait_ge(q_done, a.n(2, 2))
                dve.wait_ge(msg_done, a.n(2, 1))
                nc.vector.tensor_tensor(
                    msg[:, :, C:F].rearrange("p t (w k) -> p t k w", k=3), q[:, :, :, :],
                    msg[:, :, F:F + C].unsqueeze(2).broadcast_to([P, G, 3, C]), ALU.mult).then_inc(msg_done, 1)

            def add_window(first):
                cols = acc[0:F, bass.ds(first, WINDOW)]
                return nc.vector.tensor_tensor(cols, cols, scat_ps, ALU.add)

            def scatter(a, is_general, first=None):
                if not is_general:
                    dve.wait_ge(scat_mm, a.n(1, 1))
                    wait(dve, acc_done, a.n())
                    add_window(first).then_inc(acc_done, 1)
                    return
                dve.wait_ge(rel_done, a.n(1, 1))
                dve.sem_inc(windows_begun_dve, 1)
                with dve.Fori(0, NW) as w:
                    dve.wait_ge(scat_mm, a.n(NW, 1) + w)
                    dve.wait_ge(rel_moved, a.n(NW, 1) + w)
                    one_hot(a.par).then_inc(hot_done, 1)
                    dve.wait_ge(hot_done, a.n(NW, 1) + w)
                    nc.vector.tensor_scalar(rel[:, a.par, :], rel[:, a.par, :], -float(WINDOW), None,
                                            ALU.add).then_inc(rel_moved, 1)
                    dve.wait_ge(scat_mm, a.n(NW, 2) + w)
                    add_window(w * WINDOW).then_inc(acc_done, 1)

            def program(is_general):
                def body(at, i):
                    zero, one, two, three, four = (stage(at, by, i) for by in (2, 1, 0, -1, -2))
                    windows = NW if is_general else 1
                    if i == 0:
                        dve.wait_ge(s_length, 1)
                        inverse(0, G)
                        dve.wait_ge(s_inv, 1)
                        directions(two)
                    if two is not None:
                        vector_products(two)
                        vdots(two)
                    if four is not None:
                        messages_scalar(four, windows, int(is_general))
                    if two is not None:
                        scalar_products(two)
                    if four is not None:
                        messages_vector(four)
                        if is_general:
                            scatter(four, is_general)
                    if two is not None:
                        third_sum(two)
                    if i == 0:
                        inverse(G, G * NS)
                        dve.wait_ge(s_inv, 2)
                    if three is not None:
                        products2(three)
                    if two is not None:
                        destinations(two, is_general)
                    if four is not None and not is_general:
                        first = nc.vector.value_load(base_i[0:1, bass.ds(four.index(), 1)], min_val=0, max_val=N - 1)
                    if three is not None:
                        sums2(three)
                    if two is not None:
                        vt_first(two)
                    if three is not None:
                        q_first(three)
                    if two is not None:
                        vt_second(two)
                        st_whole(two)
                    if one is not None and i != -1:
                        directions(one)
                    if two is not None:
                        vt_dot_first(two)
                    if three is not None:
                        q_second(three)
                    if two is not None:
                        vt_dot_second(two)
                    if zero is not None:
                        split_again(zero)
                    if four is not None and not is_general:
                        scatter(four, is_general, first)
                    if two is not None and not is_general:
                        dve.wait_ge(rel_done, two.n(1, 1))
                        wait(dve, scat_mm, two.n(1, -1))
                        one_hot(two.par).then_inc(hot_done, 1)
                periods(dve, body)

            with dve.If(flag == 0):
                program(False)
            with dve.If(flag != 0):
                dve.sem_inc(acc_done, 1)
                dve.sem_inc(rel_moved, 1)
                program(True)

            after = [0]

            def then(ins):
                after[0] += 1
                ins.then_inc(post, 1)
                dve.wait_ge(post, after[0])

            then(nc.vector.memset(mean[:, :], 0.0))
            dve.wait_ge(turn_acc, 1)
            dve.wait_ge(xn_in, 32 if N > (N // NB) * NB else 16)
            banks = (pw[:, 0, 0, :], pw[:, 0, 1, :], pw[:, 1, 0, :], pw[:, 1, 1, :], ph[:, :], p1[:, :], p2[:, :])
            per = 512 // F
            for c in range(-(-NB // per)):
                n = min(per, NB - c * per)
                part = xn[:, c * per:c * per + n, :]
                ins = nc.vector.tensor_tensor(part, part, banks[c][:, 0:F * n].rearrange("p (b f) -> p b f", f=F), ALU.add)
            then(ins)
            then(nc.vector.tensor_reduce(mean[:, :], xn[:, :, :], AX.X, ALU.add))
            nc.vector.tensor_scalar(mean[:, :], mean[:, :], 1.0 / F, None, ALU.mult).then_inc(s_pre, 1)
            dve.wait_ge(s_pre, steps[0] + 1)
            then(nc.vector.tensor_tensor(xn[:, :, :], xn[:, :, :], mean[:, :].unsqueeze(2).broadcast_to([P, NB, F]),
                                         ALU.subtract))
            sq = prod_v[:, :, :, :, :].rearrange("p a b c d -> p (a b c d)")
            width = G * 3 * 2 * C * C
            assert NB * F <= 2 * width
            for c in range(2):
                b0, b1 = c * ((NB + 1) // 2), min(NB, (c + 1) * ((NB + 1) // 2))
                view = sq[:, 0:(b1 - b0) * F].rearrange("p (b f) -> p b f", f=F)
                nc.vector.tensor_tensor(view, xn[:, b0:b1, :], xn[:, b0:b1, :], ALU.mult).then_inc(s_pre, 1)
                dve.wait_ge(s_pre, steps[0] + 2 + 2 * c)
                nc.vector.tensor_reduce(var[:, b0:b1], view, AX.X, ALU.add).then_inc(s_pre, 1)
                dve.wait_ge(s_pre, steps[0] + 3 + 2 * c)
            then(nc.vector.tensor_scalar(var[:, :], var[:, :], 1.0 / F, EPS, ALU.mult, ALU.add))
            then(nc.vector.memset(mean[:, :], 0.0))
            dve.wait_ge(root_done, 1)
            then(nc.vector.reciprocal(mean[:, :], var[:, :]))
            then(nc.vector.tensor_tensor(xn[:, :, :], xn[:, :, :], mean[:, :].unsqueeze(2).broadcast_to([P, NB, F]),
                                         ALU.mult))
            then(nc.vector.memset(var[:, :], 0.0))


def kernel(x, src, dst, edge_attr_10, edge_attr_3, edge_weight,
           L0_gnn_fc1_w1, L0_gnn_fc1_w2, L0_gnn_fc2_w1, L0_gnn_fc2_w2):
    import numpy as np
    import concourse.bacc as bacc
    from concourse.bass_utils import run_bass_kernel_spmd

    nc = bacc.Bacc("TRN2", target_bir_lowering=False, num_devices=1)
    arrays = {
        "x": x, "src": src, "dst": dst, "emb_t": np.asarray(edge_attr_10).T, "vec": edge_attr_3, "weight": edge_weight,
        "fc1_w1": L0_gnn_fc1_w1, "fc1_w2": L0_gnn_fc1_w2, "fc2_w1": L0_gnn_fc2_w1, "fc2_w2": L0_gnn_fc2_w2,
    }
    arrays = {f"in_{k}": np.ascontiguousarray(v) for k, v in arrays.items()}
    args = [nc.dram_tensor(k, a.shape, mybir.dt.from_np(a.dtype), kind="ExternalInput").ap()
            for k, a in arrays.items()]
    args.append(nc.dram_tensor("out", arrays["in_x"].shape, F32, kind="ExternalOutput").ap())
    build_gnn_layer(nc, *args)
    result = run_bass_kernel_spmd(nc, [arrays], core_ids=[0])
    return result.results[0]["out"]
```
